# Optimizing a Trainium2 kernel written in Bass

```python
import numpy as np
import jax
import jax.numpy as jnp

def _softmax(x, axis=-1):
    return jax.nn.softmax(x, axis=axis)

def _gelu(x):
    return jax.nn.gelu(x, approximate=True)

def _silu(x):
    return jax.nn.silu(x)

def _sigmoid(x):
    return jax.nn.sigmoid(x)

def _layernorm(x, axis=-1, eps=1e-05):
    m = jnp.mean(x, axis=axis, keepdims=True)
    v = jnp.var(x, axis=axis, keepdims=True)
    return (x - m) / jnp.sqrt(v + eps)

def _scatter_add(tgt, idx, src, axis=0):
    return tgt.at[idx].add(src)

def _segment_sum(src, seg, n):
    return jax.ops.segment_sum(src, seg, n)
kernel_name = 'mk_seq_postln_d1_jaxref_r4_c8ba6e'

def setup_inputs(seed: int=0):
    np.random.seed(seed)
    _w = jnp.asarray

    def _L0_attn_setup():
        import jax, jax.numpy as jnp
        import numpy as np
        import math
        H = 512
        B = 4
        T = 512
        LAYER_ID = 0
        N_LAYERS = 24

        def _init_params(key):
            ratio_0_to_1 = LAYER_ID / (N_LAYERS - 1)
            ratio_1_to_0 = 1.0 - LAYER_ID / N_LAYERS
            d = jnp.arange(H, dtype=jnp.float32) / max(H - 1, 1)
            tmk = jnp.power(d, ratio_1_to_0).reshape(1, 1, H)
            tmv = jnp.clip(jnp.power(d, ratio_1_to_0) + 0.3 * ratio_0_to_1, 0.0, 1.0).reshape(1, 1, H)
            tmr = jnp.power(d, 0.5 * ratio_1_to_0).reshape(1, 1, H)
            frac = jnp.arange(H, dtype=jnp.float32) / max(H - 1, 1)
            time_decay = -5.0 + 8.0 * jnp.power(frac, 0.7 + 1.3 * ratio_0_to_1)
            zigzag = ((jnp.arange(H) + 1) % 3 - 1).astype(jnp.float32) * 0.5
            time_first = jnp.full((H,), math.log(0.3), dtype=jnp.float32) + zigzag
            ks = jax.random.split(key, 4)
            lim = math.sqrt(6.0 / (H + H))
            Wk = jax.random.uniform(ks[0], (H, H), jnp.float32, -lim, lim)
            Wv = jax.random.uniform(ks[1], (H, H), jnp.float32, -lim, lim)
            Wr = jax.random.uniform(ks[2], (H, H), jnp.float32, -lim, lim)
            Wo = jax.random.normal(ks[3], (H, H), jnp.float32) * (0.02 / math.sqrt(N_LAYERS))
            z = jnp.zeros((H,), jnp.float32)
            return dict(Wk=Wk, bk=z, Wv=Wv, bv=z, Wr=Wr, br=z, Wo=Wo, bo=z, tmk=tmk, tmv=tmv, tmr=tmr, time_decay=time_decay, time_first=time_first)

        def _wkv_scan(k, v, time_decay, time_first):
            decay = -jnp.exp(time_decay)
            bonus = time_first
            b, t, h = k.shape
            aa0 = jnp.zeros((b, h), jnp.float32)
            bb0 = jnp.zeros((b, h), jnp.float32)
            pp0 = jnp.full((b, h), -1e+30, jnp.float32)

            def step(carry, kv):
                aa, bb, pp = carry
                kt, vt = kv
                ww = bonus + kt
                p = jnp.maximum(pp, ww)
                e1 = jnp.exp(pp - p)
                e2 = jnp.exp(ww - p)
                out = (e1 * aa + e2 * vt) / (e1 * bb + e2)
                ww2 = pp + decay
                p2 = jnp.maximum(ww2, kt)
                e1 = jnp.exp(ww2 - p2)
                e2 = jnp.exp(kt - p2)
                return ((e1 * aa + e2 * vt, e1 * bb + e2, p2), out)
            kT = jnp.swapaxes(k, 0, 1)
            vT = jnp.swapaxes(v, 0, 1)
            _, outs = jax.lax.scan(step, (aa0, bb0, pp0), (kT, vT))
            return jnp.swapaxes(outs, 0, 1)
        key = jax.random.key(seed)
        kx, kp = jax.random.split(key)
        inp = {'x': jax.random.normal(kx, (B, T, H), jnp.float32)}
        inp.update(_init_params(kp))
        return inp
    _L0_attn_in = _L0_attn_setup()

    def _L0_ffn_setup():
        import jax, jax.numpy as jnp
        import numpy as np
        B, S, H, E = (4, 512, 512, 8)
        key = jax.random.key(seed)
        k_x, k_wg, k_w, k_b = jax.random.split(key, 4)
        x = jax.random.normal(k_x, (B, S, H), dtype=jnp.float32)
        wg = jax.random.normal(k_wg, (H, E), dtype=jnp.float32) * (1.0 / np.sqrt(H))
        W = jax.random.normal(k_w, (E, H, H), dtype=jnp.float32) * (1.0 / np.sqrt(H))
        b = jax.random.normal(k_b, (E, H), dtype=jnp.float32) * 0.01
        return {'x': x, 'wg': wg, 'W': W, 'b': b}
    _L0_ffn_in = _L0_ffn_setup()
    _d = {'L0_attn_x': _L0_attn_in['x'], 'L0_attn_Wk': _L0_attn_in['Wk'], 'L0_attn_bk': _L0_attn_in['bk'], 'L0_attn_Wv': _L0_attn_in['Wv'], 'L0_attn_bv': _L0_attn_in['bv'], 'L0_attn_Wr': _L0_attn_in['Wr'], 'L0_attn_br': _L0_attn_in['br'], 'L0_attn_Wo': _L0_attn_in['Wo'], 'L0_attn_bo': _L0_attn_in['bo'], 'L0_attn_tmk': _L0_attn_in['tmk'], 'L0_attn_tmv': _L0_attn_in['tmv'], 'L0_attn_tmr': _L0_attn_in['tmr'], 'L0_attn_time_decay': _L0_attn_in['time_decay'], 'L0_attn_time_first': _L0_attn_in['time_first'], 'L0_ffn_wg': _L0_ffn_in['wg'], 'L0_ffn_W': _L0_ffn_in['W'], 'L0_ffn_b': _L0_ffn_in['b']}
    _x0 = _d['L0_attn_x']
    _d['L0_attn_x'] = jax.random.normal(jax.random.fold_in(jax.random.key(seed), 1), (4, 1024, 512), dtype=_x0.dtype)
    del _x0
    return _d

def reference(L0_attn_x, L0_attn_Wk, L0_attn_bk, L0_attn_Wv, L0_attn_bv, L0_attn_Wr, L0_attn_br, L0_attn_Wo, L0_attn_bo, L0_attn_tmk, L0_attn_tmv, L0_attn_tmr, L0_attn_time_decay, L0_attn_time_first, L0_ffn_wg, L0_ffn_W, L0_ffn_b):

    def _L0_attn_ref(x, Wk, bk, Wv, bv, Wr, br, Wo, bo, tmk, tmv, tmr, time_decay, time_first):
        import jax, jax.numpy as jnp
        import numpy as np
        import math
        H = 512
        B = 4
        T = 512
        LAYER_ID = 0
        N_LAYERS = 24

        def _init_params(key):
            ratio_0_to_1 = LAYER_ID / (N_LAYERS - 1)
            ratio_1_to_0 = 1.0 - LAYER_ID / N_LAYERS
            d = jnp.arange(H, dtype=jnp.float32) / max(H - 1, 1)
            tmk = jnp.power(d, ratio_1_to_0).reshape(1, 1, H)
            tmv = jnp.clip(jnp.power(d, ratio_1_to_0) + 0.3 * ratio_0_to_1, 0.0, 1.0).reshape(1, 1, H)
            tmr = jnp.power(d, 0.5 * ratio_1_to_0).reshape(1, 1, H)
            frac = jnp.arange(H, dtype=jnp.float32) / max(H - 1, 1)
            time_decay = -5.0 + 8.0 * jnp.power(frac, 0.7 + 1.3 * ratio_0_to_1)
            zigzag = ((jnp.arange(H) + 1) % 3 - 1).astype(jnp.float32) * 0.5
            time_first = jnp.full((H,), math.log(0.3), dtype=jnp.float32) + zigzag
            ks = jax.random.split(key, 4)
            lim = math.sqrt(6.0 / (H + H))
            Wk = jax.random.uniform(ks[0], (H, H), jnp.float32, -lim, lim)
            Wv = jax.random.uniform(ks[1], (H, H), jnp.float32, -lim, lim)
            Wr = jax.random.uniform(ks[2], (H, H), jnp.float32, -lim, lim)
            Wo = jax.random.normal(ks[3], (H, H), jnp.float32) * (0.02 / math.sqrt(N_LAYERS))
            z = jnp.zeros((H,), jnp.float32)
            return dict(Wk=Wk, bk=z, Wv=Wv, bv=z, Wr=Wr, br=z, Wo=Wo, bo=z, tmk=tmk, tmv=tmv, tmr=tmr, time_decay=time_decay, time_first=time_first)

        def _wkv_scan(k, v, time_decay, time_first):
            decay = -jnp.exp(time_decay)
            bonus = time_first
            b, t, h = k.shape
            aa0 = jnp.zeros((b, h), jnp.float32)
            bb0 = jnp.zeros((b, h), jnp.float32)
            pp0 = jnp.full((b, h), -1e+30, jnp.float32)

            def step(carry, kv):
                aa, bb, pp = carry
                kt, vt = kv
                ww = bonus + kt
                p = jnp.maximum(pp, ww)
                e1 = jnp.exp(pp - p)
                e2 = jnp.exp(ww - p)
                out = (e1 * aa + e2 * vt) / (e1 * bb + e2)
                ww2 = pp + decay
                p2 = jnp.maximum(ww2, kt)
                e1 = jnp.exp(ww2 - p2)
                e2 = jnp.exp(kt - p2)
                return ((e1 * aa + e2 * vt, e1 * bb + e2, p2), out)
            kT = jnp.swapaxes(k, 0, 1)
            vT = jnp.swapaxes(v, 0, 1)
            _, outs = jax.lax.scan(step, (aa0, bb0, pp0), (kT, vT))
            return jnp.swapaxes(outs, 0, 1)
        x_prev = jnp.concatenate([jnp.zeros_like(x[:, :1, :]), x[:, :-1, :]], axis=1)
        xk = x_prev + (x - x_prev) * tmk
        xv = x_prev + (x - x_prev) * tmv
        xr = x_prev + (x - x_prev) * tmr
        k = jnp.einsum('bth,oh->bto', xk, Wk) + bk
        v = jnp.einsum('bth,oh->bto', xv, Wv) + bv
        r = jnp.einsum('bth,oh->bto', xr, Wr) + br
        wkv = _wkv_scan(k, v, time_decay, time_first)
        rwkv = jax.nn.sigmoid(r) * wkv
        out = jnp.einsum('bth,oh->bto', rwkv, Wo) + bo
        return out

    def _L0_ffn_ref(x, wg, W, b):
        import jax, jax.numpy as jnp
        import numpy as np
        B, S, H, E = (4, 512, 512, 8)
        Bv, Sv, Hv = x.shape
        Ev = W.shape[0]
        xt = x.reshape(-1, Hv)
        logits = xt @ wg
        probs = jax.nn.softmax(logits, axis=-1)
        idx = jnp.argmax(probs, axis=-1)
        gate = jnp.take_along_axis(probs, idx[:, None], axis=1)
        onehot = jax.nn.one_hot(idx, Ev, dtype=x.dtype)
        expert_out = jnp.einsum('nh,eoh->neo', xt, W) + b[None, :, :]
        combine = onehot * gate
        out = jnp.einsum('ne,neo->no', combine, expert_out)
        return out.reshape(Bv, Sv, Hv)
    x = L0_attn_x
    x = _layernorm(x + _L0_attn_ref(x, L0_attn_Wk, L0_attn_bk, L0_attn_Wv, L0_attn_bv, L0_attn_Wr, L0_attn_br, L0_attn_Wo, L0_attn_bo, L0_attn_tmk, L0_attn_tmv, L0_attn_tmr, L0_attn_time_decay, L0_attn_time_first), axis=-1)
    x = _layernorm(x + _L0_ffn_ref(x, L0_ffn_wg, L0_ffn_W, L0_ffn_b), axis=-1)
    return x

_drawn_inputs = setup_inputs


def setup_inputs(seed=0):
    import zlib

    import numpy as np

    out = dict(_drawn_inputs(seed))
    spreads = {'L0_attn_bk': (0.0, 2.0),
     'L0_attn_bv': (0.0, 0.305),
     'L0_attn_br': (0.0, 2.0),
     'L0_attn_bo': (0.0, 0.1)}
    factors = {'L0_attn_tmr': 3.169, 'L0_attn_time_first': 64.0, 'L0_ffn_b': 8.0, 'L0_attn_tmk': 2.701}
    for name, (base, spread) in spreads.items():
        noise = np.random.default_rng([zlib.crc32(name.encode()), seed]).standard_normal(out[name].shape)
        drawn = base * np.exp(spread * noise) if base else spread * noise
        out[name] = jnp.asarray(drawn.astype(out[name].dtype))
    for name, factor in factors.items():
        out[name] = (out[name] * factor).astype(out[name].dtype)
    return out
```

```python
from contextlib import ExitStack

import concourse.bass as bass
from concourse import mybir

ALU = mybir.AluOpType
ACT = mybir.ActivationFunctionType
AX_X = mybir.AxisListType.X
F32 = mybir.dt.float32
F32R = mybir.dt.float32r
I32 = mybir.dt.int32
U32 = mybir.dt.uint32

P = 128
BATCH, TIME, H = 4, 1024, 512
EXPERTS = 8
CH = H // P
TB = 512
HALVES = TIME // TB
BLOCKS = BATCH * HALVES
PAIRS = CH // 2
SLOTS = BLOCKS * PAIRS
TPB = TB // P
TOKENS = BATCH * TIME
TILES = TOKENS // P
SORTED = TILES + EXPERTS - 1
RING = 4
EPS = 1e-5
EXPONENT_CAP = 27.0
SIGMOID_CAP = 2.0 ** 80
LN_SHIFT = 60
LN2 = 0.6931471805599453
START = -1e30
K, V, R, O = range(4)
HI, LO = range(2)
SQ, SA, SB = range(3)
BIAS_ROWS = 2 * EXPERTS + 2
VEC_BK, VEC_BV, VEC_BR, VEC_MK, VEC_MV, VEC_MR, VEC_DECAY, VEC_FIRST = range(8)


def wait(eng, sem, value):
    if not isinstance(value, int) or value > 0:
        eng.wait_ge(sem, value)


class Slot:

    def __init__(self, g, batch, i, p, half, first=False, has_prev_block=True, has_next_block=True):
        self.g, self.batch, self.i, self.p, self.half = g, batch, i, p, half
        self.first, self.has_prev_block, self.has_next_block = first, has_prev_block, has_next_block


def walk(eng, slot, block_loop):
    slot(Slot(0, 0, 0, 0, 0, first=True, has_prev_block=False))
    slot(Slot(1, 0, 0, 1, 0, has_prev_block=False))
    with block_loop(0, BATCH - 1) as b:
        for s in range(4):
            slot(Slot(b * 4 + (2 + s), b + s // 2, b * 2 + (1 + s // 2), s % 2, (1 + s // 2) % 2))
    slot(Slot(SLOTS - 2, BATCH - 1, BLOCKS - 1, 0, 1))
    slot(Slot(SLOTS - 1, BATCH - 1, BLOCKS - 1, 1, 1, has_next_block=False))


def build(nc, x, xT, w_square, w_experts, vectors, bo, b_experts, wg, out):
    x1_rows = nc.dram_tensor("x1_rows", [TOKENS + 1, H], F32, kind="Internal").ap()

    with ExitStack() as ctx:
        cursor = [0]

        def place(name, shape, dtype, at=None):
            size = 4
            for n in shape[1:]:
                size *= n
            size = (size + 31) // 32 * 32
            offset = cursor[0] if at is None else at
            if at is None:
                cursor[0] += size
            return nc.alloc_sbuf_tensor_at(name, shape, dtype, offset=offset)

        base = nc.sbuf_base + (-nc.sbuf_base) % 32
        cursor[0] = base
        mat = 2 * CH * H * 4
        w_kvr = place("w_kvr", [P, 3, 2, CH, H], F32R)
        mixed = place("mixed", [P, 3, 2, CH, TB], F32R)
        w_o = place("w_o", [P, 2, CH, H], F32R)
        rw = place("rw", [P, 2, CH, TB], F32R)
        w_e_bytes = EXPERTS * mat
        diff_at = cursor[0]
        diff = place("diff", [P, CH, TB], F32)
        mix_at = cursor[0]
        mix = place("mix", [P, 2, 2, TB], F32)
        xb_at = cursor[0]
        xb = place("xb", [P, CH, TB + 1], F32)
        temps_at = cursor[0]
        kd = place("kd", [P, 2, 2, TB], F32)
        vn = place("vn", [P, 2, 2, TB], F32)
        er = place("er", [P, 2, TB], F32)
        state = place("state", [P, 3, 2, TB + 1], F32)
        e12 = place("e12", [P, 2, 2, TB], F32)
        rows_at = cursor[0]
        rows = place("rows", [P, TPB, H], F32)
        x1T = place("x1T", [P, CH, P], F32)
        bias_rows = place("bias_rows", [BIAS_ROWS, H], F32R)
        sel_bo = place("sel_bo", [BIAS_ROWS, P], F32R)
        ident = place("ident", [P, P], F32)
        vec = place("vec", [P, 8, CH], F32)
        wgs = place("wgs", [P, CH, EXPERTS], F32)
        wdec = place("wdec", [P, CH], F32)
        uw = place("uw", [P, CH], F32)
        nbr = place("nbr", [P, CH], F32)
        start_state = place("start_state", [P, 3, 2], F32)
        carry = place("carry", [P, 2, 3, 2], F32)
        bn = place("bn", [P, TPB, 6], F32)
        stats = place("stats", [P, TPB, 2], F32)
        rstd = place("rstd", [P, TPB], F32)
        nmr = place("nmr", [P, TPB], F32)
        eps_t = place("eps_t", [P, 1], F32)
        cap_t = place("cap_t", [P, 1], F32)
        part = place("part", [P, 1], F32)
        part8 = place("part8", [P, 1], F32)
        assert cursor[0] <= nc.sbuf_usable_end, cursor[0]
        w_raw = place("w_raw", [P, CH, CH, H], F32, at=temps_at)
        raw_at = temps_at + 4 * CH * CH * H
        b_raw = place("b_raw", [EXPERTS, H], F32, at=raw_at)
        b_split = place("b_split", [EXPERTS, 2, H], F32R, at=raw_at + 4 * H)
        bo_raw = place("bo_raw", [1, H], F32, at=raw_at + 4 * 3 * H)
        assert raw_at + 4 * 4 * H <= rows_at
        bo_split = place("bo_split", [1, 2, H], F32R, at=rows_at)
        zero_row = place("zero_row", [1, H], F32, at=rows_at + 4 * 2 * H)
        w_e = place("w_e", [P, EXPERTS, 2, CH, H], F32R, at=base)
        assert w_e_bytes == diff_at - base
        we_raw = [place(f"we_raw{n}", [P, CH, H], F32, at=at) for n, at in enumerate((diff_at, xb_at))]
        cursor[0] = mix_at
        before = place("before", [P, P], F32)
        ones = place("ones", [P, P], F32)
        iota_q = place("iota_q", [P, P], F32)
        segment = place("segment", [P, EXPERTS, TILES], F32)
        steps = place("steps", [P, EXPERTS, TILES], F32)
        iota_k = place("iota_k", [P, SORTED], F32)
        token1 = place("token1", [P, TILES], F32)
        rank8 = place("rank8", [P, EXPERTS], F32)
        assert cursor[0] <= mix_at + 4 * 4 * TB
        cursor[0] = temps_at
        place_q = place("place_q", [P, TILES, P], F32)
        place_k = place("place_k", [P, TILES, 2, SORTED], F32)
        xg = place("xg", [P, RING, H], F32)
        assert cursor[0] <= rows_at
        xgT = place("xgT", [P, 2, 2, CH, P], F32R, at=temps_at)
        cursor[0] = rows_at
        lg = place("lg", [P, TILES, EXPERTS], F32)
        hot = place("hot", [P, EXPERTS, TILES], F32)
        work = place("work", [P, EXPERTS, TILES], F32)
        place_e = place("place_e", [P, EXPERTS, TILES], F32)
        mx = place("mx", [P, TILES], F32)
        chosen = place("chosen", [P, TILES], F32)
        sums = place("sums", [P, TILES], F32)
        gate = place("gate", [P, TILES], F32)
        dest = place("dest", [P, TILES], F32)
        dest_i = place("dest_i", [P, 3, TILES], I32)
        dest_f = place("dest_f", [P, 2, TILES], F32)
        ntiles = place("ntiles", [P, EXPERTS], F32)
        ends = place("ends", [P, EXPERTS], F32)
        starts = place("starts", [P, EXPERTS], F32)
        after = place("after", [P, SORTED, EXPERTS], F32)
        tile_e = place("tile_e", [P, SORTED], F32)
        tile_ei = place("tile_ei", [P, SORTED], I32)
        gates = place("gates", [P, SORTED], F32)
        empty = place("empty", [P, SORTED], F32)
        ids = place("ids", [P, SORTED], U32)
        id_now = place("id_now", [P, RING, 1], U32)
        bn2 = place("bn2", [P, RING, 6], F32)
        stats2 = place("stats2", [P, RING, 2], F32)
        rstd2 = place("rstd2", [P, RING], F32)
        nmr2 = place("nmr2", [P, RING], F32)
        sel_e = place("sel_e", [BIAS_ROWS, 2, P], F32R)
        assert cursor[0] <= rows_at + 4 * (TPB * H + CH * P), cursor[0] - rows_at

        proj = ctx.enter_context(nc.psum_tensor("proj", [P, 4, TB], F32))
        y_ps = ctx.enter_context(nc.psum_tensor("y_ps", [P, 2, H], F32))
        t_ps = ctx.enter_context(nc.psum_tensor("t_ps", [P, CH, P], F32))
        lg_ps = ctx.enter_context(nc.psum_tensor("lg_ps", [P, TILES, EXPERTS], F32))

        def sem(name):
            return ctx.enter_context(nc.semaphore(name))

        waits_passed = sem("waits_passed")
        vec_loaded, w_loaded = sem("vec_loaded"), [sem(f"w_loaded{n}") for n in range(4)]
        b_loaded, bias_moved, zero_stored = sem("b_loaded"), sem("bias_moved"), sem("zero_stored")
        consts_set, decay_exp, vec_ready = sem("consts_set"), sem("decay_exp"), sem("vec_ready")
        w_hi, w_lo, b_hi, b_lo = sem("w_hi"), sem("w_lo"), sem("b_hi"), sem("b_lo")
        ident_zero, ident_ready, sel_ready = sem("ident_zero"), sem("ident_ready"), sem("sel_ready")
        x_loaded, x_padded, diffed, mixed_f32 = sem("x_loaded"), sem("x_padded"), sem("diffed"), sem("mixed_f32")
        mixed_hi, mixed_lo = sem("mixed_hi"), sem("mixed_lo")
        proj_filled, proj_moved = sem("proj_filled"), sem("proj_moved")
        state_in, maxed, d_ready, capped = sem("state_in"), sem("maxed"), sem("d_ready"), sem("capped")
        clipped, e12_ready, big_e = sem("clipped"), sem("e12_ready"), sem("big_e")
        b_scanned, a_scanned, carried = sem("b_scanned"), sem("a_scanned"), sem("carried")
        ev_ready, big_ev, r_capped = sem("ev_ready"), sem("big_ev"), sem("r_capped")
        num_ready, den_part, den_ready = sem("num_ready"), sem("den_part"), sem("den_ready")
        den_ln, recip_guess, newton = sem("den_ln"), sem("recip_guess"), sem("newton")
        wkv_done, rw_hi, rw_lo = sem("wkv_done"), sem("rw_hi"), sem("rw_lo")
        row_loaded = [sem(f"row_loaded{j}") for j in range(TPB)]
        row_stored = [sem(f"row_stored{j}") for j in range(TPB)]
        y_filled, y_taken, bn_done, stats_done = sem("y_filled"), sem("y_taken"), sem("bn_done"), sem("stats_done")
        row_turned, x1T_moved = sem("row_turned"), sem("x1T_moved")
        var_ln, rstd_ready, nmr_ready, x1_ready = sem("var_ln"), sem("rstd_ready"), sem("nmr_ready"), sem("x1_ready")
        logits_done = sem("logits_done")
        route_const, routed, hot_ready, shifted = sem("route_const"), sem("routed"), sem("hot_ready"), sem("shifted")
        gate_exp, counted, placed, listed = sem("gate_exp"), sem("counted"), sem("placed"), sem("listed")
        ids_ready, tiles_ready = sem("ids_ready"), sem("tiles_ready")
        we_loaded = [sem(f"we_loaded{n}") for n in range(2)]
        we_hi, we_lo = sem("we_hi"), sem("we_lo")
        id_set, gathered = sem("id_set"), [sem(f"gathered{n}") for n in range(RING)]
        turned, turned_hi, turned_lo, sel_set = sem("turned"), sem("turned_hi"), sem("turned_lo"), sem("sel_set")
        expert_filled, bn2_done, stats2_done = sem("expert_filled"), sem("bn2_done"), sem("stats2_done")
        var2_ln, rstd2_ready, nmr2_ready, out_ready = (
            sem("var2_ln"), sem("rstd2_ready"), sem("nmr2_ready"), sem("out_ready"))
        scattered = [sem(f"scattered{n}") for n in range(RING)]

        def wait_apart(eng, sem, value):
            if not isinstance(value, int) or value > 0:
                eng.wait_ge(sem, value)
                if not isinstance(value, int):
                    eng.sem_inc(waits_passed, 1)

        block = ctx.enter_context(nc.Block())

        xT_v = xT.rearrange("b (c p) t -> b p c t", p=P)
        x_v = x.rearrange("b (n p) h -> (b n) p h", p=P)
        x1_v = x1_rows[0:TOKENS, :].rearrange("(n p) h -> n p h", p=P)
        w_v = w_square.rearrange("m (c p) o -> m p c o", p=P)
        we_v = w_experts.rearrange("e (c p) o -> e p c o", p=P)
        out_v = out.rearrange("b t h -> (b t) h")

        @block.sync
        def _(sp):
            sp.dma_start(vec[:], vectors).then_inc(vec_loaded, 16)
            sp.dma_start(w_raw[:, K], w_v[K]).then_inc(w_loaded[K], 16)

            def load_x(n, half):
                wait(sp, mixed_f32, n * 6)
                if half == 0:
                    sp.dma_start(xb[:, :, 1:], xT_v[n // 2, :, :, 0:TB]).then_inc(x_loaded, 16)
                else:
                    sp.dma_start(xb[:], xT_v[n // 2, :, :, TB - 1:]).then_inc(x_loaded, 16)

            def load_rows(n, first):
                for j in range(TPB):
                    if not first:
                        wait_apart(sp, row_turned, n * TPB + (j + 1 - TPB))
                        wait_apart(sp, row_stored[j], n * 16)
                    sp.dma_start(rows[:, j], x_v[n * TPB + j]).then_inc(row_loaded[j], 16)

            def store_rows(n):
                for j in range(TPB):
                    wait_apart(sp, x1_ready, n * TPB + (j + 1))
                    sp.dma_start(x1_v[n * TPB + j], rows[:, j]).then_inc(row_stored[j], 16)

            load_x(0, 0)
            for n in (V, R, O):
                sp.dma_start(w_raw[:, n], w_v[n]).then_inc(w_loaded[n], 16)
            sp.dma_start(b_raw[:], b_experts).then_inc(b_loaded, 16)
            sp.dma_start(bo_raw[:], bo).then_inc(b_loaded, 16)
            sp.dma_start(wgs[:], wg.rearrange("(c p) e -> p c e", p=P)).then_inc(b_loaded, 16)
            sp.wait_ge(consts_set, 1)
            sp.dma_start(x1_rows[TOKENS:TOKENS + 1, :], zero_row[:]).then_inc(zero_stored, 16)
            sp.wait_ge(b_lo, 2)
            for s in range(2):
                sp.dma_start(bias_rows[s * EXPERTS:(s + 1) * EXPERTS, :].bitcast(F32), b_split[:, s, :].bitcast(F32)).then_inc(bias_moved, 16)
                sp.dma_start(bias_rows[2 * EXPERTS + s:2 * EXPERTS + s + 1, :].bitcast(F32), bo_split[:, s, :].bitcast(F32)).then_inc(bias_moved, 16)
            sp.wait_ge(bias_moved, 64)
            sp.wait_ge(zero_stored, 16)
            load_x(1, 1)
            load_rows(0, first=True)
            with sp.Fori(0, BATCH - 1) as b:
                store_rows(b * 2)
                wait_apart(sp, mixed_f32, b * 12 + 12)
                sp.dma_start(xb[:, :, 1:], xT_v[b + 1, :, :, 0:TB]).then_inc(x_loaded, 16)
                load_rows(b * 2 + 1, first=False)
                store_rows(b * 2 + 1)
                wait_apart(sp, mixed_f32, b * 12 + 18)
                sp.dma_start(xb[:], xT_v[b + 1, :, :, TB - 1:]).then_inc(x_loaded, 16)
                load_rows(b * 2 + 2, first=False)
            store_rows(BLOCKS - 2)
            load_rows(BLOCKS - 1, first=False)
            sp.wait_ge(mixed_f32, BLOCKS * 6)
            for e in range(2):
                sp.dma_start(we_raw[e][:], we_v[e]).then_inc(we_loaded[e], 16)
            store_rows(BLOCKS - 1)
            for e in range(2, EXPERTS):
                sp.wait_ge(we_lo, e - 1)
                sp.dma_start(we_raw[e % 2][:], we_v[e]).then_inc(we_loaded[e % 2], 16)

        @block.tensor
        def _(pe):
            def project(s, m):
                if s.p == 0:
                    pe.wait_ge(mixed_lo, s.i * 6 + (2 * m + 2))
                for c in range(2):
                    n = 2 * m + c
                    bank = (6 * s.p + n) % 4
                    wait(pe, proj_moved, s.g * 6 + (n - 3))
                    o = (2 * s.p + c) * P
                    k = 0
                    for h in range(CH):
                        for a, bb in ((HI, HI), (HI, LO), (LO, HI)):
                            mm = pe.matmul(proj[:, bank, :], w_kvr[:, m, a, h, o:o + P], mixed[:, m, bb, h, :],
                                           start=(k == 0), stop=(k == 3 * CH - 1))
                            k += 1
                    mm.then_inc(proj_filled, 1)

            def project_out(n, j):
                pe.wait_ge(rw_lo, n * 2 + 2)
                pe.wait_ge(y_taken, n * TPB + (j + 1))
                pe.matmul(y_ps[:, j % 2, :], sel_bo[:], bias_rows[:], start=True, stop=False)
                for c in range(CH):
                    for a, bb in ((HI, HI), (HI, LO), (LO, HI)):
                        mm = pe.matmul(y_ps[:, j % 2, :], rw[:, a, c, j * P:(j + 1) * P], w_o[:, bb, c, :],
                                       start=False, stop=(c == CH - 1 and (a, bb) == (LO, HI)))
                mm.then_inc(y_filled, 1)

            def turn_rows(n, j):
                pe.wait_ge(x1_ready, n * TPB + (j + 1))
                for c in range(CH):
                    mm = pe.transpose(t_ps[:, c, :], rows[:, j, c * P:(c + 1) * P], ident[:])
                mm.then_inc(row_turned, 1)

            def logits(n, j, tile):
                pe.wait_ge(x1T_moved, n * TPB + (j + 1))
                for c in range(CH):
                    mm = pe.matmul(lg_ps[:, tile, :], x1T[:, c, :], wgs[:, c, :], start=(c == 0), stop=(c == CH - 1))
                mm.then_inc(logits_done, 1)

            def slot(s):
                if s.first:
                    pe.wait_ge(w_lo, K + 1)
                turning = s.p == 1 and s.has_prev_block
                for m in (K, V, R):
                    if s.first:
                        pe.wait_ge(w_lo, m + 1)
                    if turning:
                        if m:
                            logits(s.i - 1, m - 1, (s.i - 1) * TPB + (m - 1))
                        turn_rows(s.i - 1, m)
                    project(s, m)
                if turning:
                    logits(s.i - 1, 2, (s.i - 1) * TPB + 2)
                    turn_rows(s.i - 1, 3)
                    logits(s.i - 1, 3, (s.i - 1) * TPB + 3)
                if s.p == 0 and s.has_prev_block:
                    for j in range(TPB):
                        project_out(s.i - 1, j)

            pe.wait_ge(sel_ready, 1)
            pe.wait_ge(ident_ready, 1)
            pe.wait_ge(bias_moved, 64)
            pe.wait_ge(b_loaded, 48)
            walk(pe, slot, pe.Fori)
            last = BLOCKS - 1
            for j in range(TPB):
                project_out(last, j)
            for j in range(TPB):
                turn_rows(last, j)
                logits(last, j, last * TPB + j)

            n_te = EXPERTS * TILES
            pe.wait_ge(route_const, 1)
            pe.wait_ge(hot_ready, 1)
            hot_all = hot[:].rearrange("p e t -> p (e t)")
            pe.matmul(y_ps[:, 0, 0:n_te], before[:], hot_all, start=True, stop=True)
            pe.matmul(y_ps[:, 1, 0:n_te], ones[:], hot_all, start=True, stop=True).then_inc(counted, 1)
            pe.wait_ge(placed, 1)
            list_ps = t_ps[:].rearrange("p c q -> p (c q)")[:, 0:2 * SORTED]
            for t in range(TILES):
                mm = pe.matmul(list_ps, place_q[:, t, :], place_k[:, t].rearrange("p w k -> p (w k)"),
                               start=(t == 0), stop=(t == TILES - 1))
            mm.then_inc(listed, 1)

            def turn(k, r, n):
                pe.wait_ge(gathered[n], r * 16 + 16)
                wait(pe, turned_lo, k)
                for c in range(CH):
                    mm = pe.transpose(t_ps[:, c, :], xg[:, n, c * P:(c + 1) * P], ident[:])
                mm.then_inc(turned, 1)

            def expert(k, parity):
                e = pe.value_load(tile_ei[0:1, bass.ds(k, 1)], min_val=0, max_val=EXPERTS - 1)
                pe.wait_ge(turned_lo, k + 1)
                pe.wait_ge(sel_set, k + 1)
                pe.wait_ge(y_taken, k + (TILES + 1))
                pe.matmul(y_ps[:, parity, :], sel_e[:, parity, :], bias_rows[:], start=True, stop=False)
                for c in range(CH):
                    for a, bb in ((HI, HI), (HI, LO), (LO, HI)):
                        mm = pe.matmul(y_ps[:, parity, :], xgT[:, parity, a, c, :],
                                       w_e[:, bass.ds(e, 1), bb, c, :].rearrange("p u o -> p (u o)"),
                                       start=False, stop=(c == CH - 1 and (a, bb) == (LO, HI)))
                mm.then_inc(expert_filled, 1)

            pe.wait_ge(tiles_ready, 1)
            pe.wait_ge(ids_ready, 1)
            pe.wait_ge(we_lo, EXPERTS)
            turn(0, 0, 0)
            turn(1, 0, 1)
            expert(0, 0)
            with pe.Fori(0, (SORTED - 3) // RING) as r:
                for n in range(RING):
                    k = n + 2
                    turn(r * RING + k, r + k // RING, k % RING)
                    expert(r * RING + (n + 1), (n + 1) % 2)
            turn(SORTED - 1, (SORTED - 1) // RING, (SORTED - 1) % RING)
            expert(SORTED - 2, SORTED % 2)
            expert(SORTED - 1, (SORTED - 1) % 2)

        @block.scalar
        def _(act):
            def mix_hi(n, m, first=False):
                for hp in range(2):
                    act.wait_ge(mixed_f32, n * 6 + (2 * m + hp + 1))
                    if not first and hp == 0:
                        act.wait_ge(proj_filled, n * 12 + (2 * m - 4))
                    act.activation(mixed[:, m, HI, 2 * hp:2 * hp + 2, :], mix[:, hp], ACT.Copy).then_inc(mixed_hi, 1)

            def evacuate(s, m):
                for c in range(2):
                    n = 2 * m + c
                    bank = (6 * s.p + n) % 4
                    act.wait_ge(proj_filled, s.g * 6 + (n + 1))
                    col = slice(2 * s.p + c, 2 * s.p + c + 1)
                    if m == K:
                        wait(act, wkv_done, s.g - 1)
                        ins = act.activation(kd[:, s.p, c, :], proj[:, bank, :], ACT.Identity, bias=vec[:, VEC_BK, col])
                    elif m == V:
                        wait(act, rw_lo, s.g - 1)
                        ins = act.activation(vn[:, s.p, c, :], proj[:, bank, :], ACT.Identity, bias=vec[:, VEC_BV, col])
                    else:
                        wait(act, wkv_done, s.g)
                        ins = act.activation(er[:, c, :], proj[:, bank, :], ACT.Exp, bias=nbr[:, col], scale=-1.0)
                    ins.then_inc(proj_moved, 1)

            def rwkv_hi(g, i, p):
                act.wait_ge(wkv_done, g + 1)
                if p == 0:
                    wait(act, y_filled, i * TPB)
                act.activation(rw[:, HI, 2 * p:2 * p + 2, :], vn[:, p], ACT.Copy).then_inc(rw_hi, 1)

            def reciprocal_guess(s):
                act.wait_ge(den_ready, s.g + 1)
                act.activation(er[:], kd[:, s.p], ACT.Ln, scale=2.0 ** -LN_SHIFT).then_inc(den_ln, 1)
                act.wait_ge(den_ln, s.g + 1)
                act.activation(er[:], er[:], ACT.Exp, bias=cap_t[:], scale=-1.0).then_inc(recip_guess, 1)

            def norm(n):
                act.wait_ge(stats_done, n * TPB + TPB)
                act.activation(rstd[:], stats[:, :, 1], ACT.Ln, bias=eps_t[:]).then_inc(var_ln, 1)
                act.wait_ge(var_ln, n + 1)
                act.activation(rstd[:], rstd[:], ACT.Exp, scale=-0.5).then_inc(rstd_ready, 1)
                act.wait_ge(nmr_ready, n + 1)
                for j in range(TPB):
                    act.activation(rows[:, j], rows[:, j], ACT.Identity, bias=nmr[:, j:j + 1],
                                   scale=rstd[:, j:j + 1]).then_inc(x1_ready, 1)

            def move_turned(n, j):
                act.wait_ge(row_turned, n * TPB + (j + 1))
                act.activation(x1T[:], t_ps[:], ACT.Copy).then_inc(x1T_moved, 1)

            def slot(s):
                turning = s.p == 1 and s.has_prev_block
                mixing = s.p == 1 and s.has_next_block
                if turning:
                    move_turned(s.i - 1, 0)
                evacuate(s, K)
                if turning:
                    move_turned(s.i - 1, 1)
                evacuate(s, V)
                if mixing:
                    mix_hi(s.i + 1, K)
                act.wait_ge(clipped, s.g * 2 + 1)
                act.activation(e12[:, 0], e12[:, 0], ACT.Exp).then_inc(e12_ready, 1)
                act.wait_ge(clipped, s.g * 2 + 2)
                act.activation(e12[:, 1], e12[:, 1], ACT.Exp, scale=-1.0).then_inc(e12_ready, 1)
                if not s.first:
                    rwkv_hi(s.g - 1, s.i - (1 - s.p), 1 - s.p)
                if mixing:
                    mix_hi(s.i + 1, V)
                act.wait_ge(capped, s.g * 2 + 2)
                act.activation(kd[:, s.p], kd[:, s.p], ACT.Exp, scale=-1.0).then_inc(big_e, 1)
                evacuate(s, R)
                if turning:
                    move_turned(s.i - 1, 2)
                if mixing:
                    mix_hi(s.i + 1, R)
                if turning:
                    move_turned(s.i - 1, 3)
                if s.p == 0 and s.has_prev_block:
                    norm(s.i - 1)
                reciprocal_guess(s)

            act.preload_act_table_set("natural_log_exp_and_others")
            act.wait_ge(vec_loaded, 16)
            act.activation(wdec[:], vec[:, VEC_DECAY, :], ACT.Exp).then_inc(decay_exp, 1)
            for m in (K, V, R, O):
                act.wait_ge(w_loaded[m], 16)
                if m == V:
                    for mm in (K, V, R):
                        mix_hi(0, mm, first=True)
                dst = w_o[:, HI] if m == O else w_kvr[:, m, HI]
                act.activation(dst, w_raw[:, m], ACT.Copy).then_inc(w_hi, 1)
            act.wait_ge(b_loaded, 48)
            act.activation(b_split[:, HI], b_raw[:], ACT.Copy).then_inc(b_hi, 1)
            act.activation(bo_split[:, HI], bo_raw[:], ACT.Copy).then_inc(b_hi, 1)
            act.wait_ge(consts_set, 1)
            act.wait_ge(w_lo, 4)
            walk(act, slot, act.Fori)
            last = BLOCKS - 1
            rwkv_hi(SLOTS - 1, last, 1)

            def expert_hi(e):
                act.wait_ge(we_loaded[e % 2], e // 2 * 16 + 16)
                act.activation(w_e[:, e, HI], we_raw[e % 2][:], ACT.Copy).then_inc(we_hi, 1)

            act.wait_ge(proj_filled, SLOTS * 6)
            expert_hi(0)
            expert_hi(1)
            norm(last)
            for j in range(TPB):
                move_turned(last, j)
            for e in range(2, EXPERTS - 2):
                expert_hi(e)
            act.wait_ge(hot_ready, 1)
            act.activation(lg[:], lg[:], ACT.Exp).then_inc(gate_exp, 1)
            act.wait_ge(y_filled, TILES)
            for e in range(EXPERTS - 2, EXPERTS):
                expert_hi(e)

            def turned_split_hi(k, parity):
                act.wait_ge(turned, k + 1)
                wait(act, expert_filled, k - 1)
                act.activation(xgT[:, parity, HI], t_ps[:], ACT.Copy).then_inc(turned_hi, 1)

            def norm2(k, n):
                act.wait_ge(stats2_done, k + 1)
                act.activation(rstd2[:, n:n + 1], stats2[:, n, 1:2], ACT.Ln, bias=eps_t[:]).then_inc(var2_ln, 1)
                act.wait_ge(var2_ln, k + 1)
                act.activation(rstd2[:, n:n + 1], rstd2[:, n:n + 1], ACT.Exp, scale=-0.5).then_inc(rstd2_ready, 1)
                act.wait_ge(nmr2_ready, k + 1)
                act.activation(xg[:, n], xg[:, n], ACT.Identity, bias=nmr2[:, n:n + 1],
                               scale=rstd2[:, n:n + 1]).then_inc(out_ready, 1)

            act.wait_ge(listed, 1)
            turned_split_hi(0, 0)
            turned_split_hi(1, 1)
            with act.Fori(0, (SORTED - 3) // RING) as r:
                for n in range(RING):
                    turned_split_hi(r * RING + (n + 2), n % 2)
                    norm2(r * RING + n, n)
            turned_split_hi(SORTED - 1, (SORTED - 1) % 2)
            for k in range(SORTED - 3, SORTED):
                norm2(k, k % RING)

        @block.gpsimd
        def _(pool):
            def mix_lo(n, m):
                for hp in range(2):
                    pool.wait_ge(mixed_hi, n * 6 + (2 * m + hp + 1))
                    pool.tensor_tensor(mixed[:, m, LO, 2 * hp:2 * hp + 2, :], mix[:, hp],
                                       mixed[:, m, HI, 2 * hp:2 * hp + 2, :].bitcast(F32),
                                       ALU.subtract).then_inc(mixed_lo, 1)

            def rwkv_lo(g, p):
                pool.wait_ge(rw_hi, g + 1)
                pool.tensor_tensor(rw[:, LO, 2 * p:2 * p + 2, :], vn[:, p],
                                   rw[:, HI, 2 * p:2 * p + 2, :].bitcast(F32), ALU.subtract).then_inc(rw_lo, 1)

            def slot(s):
                mixing = s.p == 1 and s.has_next_block
                if mixing:
                    mix_lo(s.i + 1, K)
                if not s.first:
                    rwkv_lo(s.g - 1, 1 - s.p)
                if mixing:
                    mix_lo(s.i + 1, V)
                pool.wait_ge(b_scanned, s.g * 2 + 2)
                pool.wait_ge(proj_moved, s.g * 6 + 4)
                pool.tensor_tensor(e12[:, 1], e12[:, 1], vn[:, s.p], ALU.mult).then_inc(ev_ready, 1)
                pool.wait_ge(big_e, s.g + 1)
                pool.wait_ge(ev_ready, s.g + 1)
                pool.tensor_tensor(vn[:, s.p], vn[:, s.p], kd[:, s.p], ALU.mult).then_inc(big_ev, 1)
                if mixing:
                    mix_lo(s.i + 1, R)

            pool.memset(ident[:], 0.0).then_inc(ident_zero, 1)
            pool.wait_ge(ident_zero, 1)
            pool.affine_select(out=ident[:], in_=ident[:], compare_op=ALU.not_equal, fill=1.0, base=0,
                               pattern=[[-1, P]], channel_multiplier=1).then_inc(ident_ready, 1)
            pool.iota(part[:], pattern=[[0, 1]], base=0, channel_multiplier=1,
                      allow_small_or_imprecise_dtypes=True).then_inc(ident_zero, 1)
            for m in (K, V, R, O):
                if m == V:
                    for mm in (K, V, R):
                        mix_lo(0, mm)
                pool.wait_ge(w_hi, m + 1)
                hi, lo = (w_o[:, HI], w_o[:, LO]) if m == O else (w_kvr[:, m, HI], w_kvr[:, m, LO])
                pool.tensor_tensor(lo, w_raw[:, m], hi.bitcast(F32), ALU.subtract).then_inc(w_lo, 1)
            pool.wait_ge(b_hi, 2)
            pool.tensor_tensor(b_split[:, LO], b_raw[:], b_split[:, HI].bitcast(F32), ALU.subtract).then_inc(b_lo, 1)
            pool.tensor_tensor(bo_split[:, LO], bo_raw[:], bo_split[:, HI].bitcast(F32), ALU.subtract).then_inc(b_lo, 1)
            walk(pool, slot, pool.Fori)
            rwkv_lo(SLOTS - 1, 1)

            rc = []
            rc.append(pool.memset(before[:], 1.0))
            rc.append(pool.memset(ones[:], 1.0))
            rc.append(pool.memset(segment[:], 1.0))
            rc.append(pool.iota(iota_q[:], pattern=[[1, P]], base=0, channel_multiplier=0, allow_small_or_imprecise_dtypes=True))
            rc.append(pool.iota(steps[:], pattern=[[0, EXPERTS], [P, TILES]], base=0, channel_multiplier=0, allow_small_or_imprecise_dtypes=True))
            rc.append(pool.iota(iota_k[:], pattern=[[1, SORTED]], base=0, channel_multiplier=0, allow_small_or_imprecise_dtypes=True))
            rc.append(pool.iota(token1[:], pattern=[[P, TILES]], base=1, channel_multiplier=1, allow_small_or_imprecise_dtypes=True))
            rc.append(pool.iota(rank8[:], pattern=[[-1, EXPERTS]], base=EXPERTS, channel_multiplier=0, allow_small_or_imprecise_dtypes=True))
            rc[-1].then_inc(ident_zero, 1)
            pool.wait_ge(ident_zero, 3)
            pool.memset(segment[:, :, 0:1], 0.0)
            pool.affine_select(out=before[:], in_=before[:], compare_op=ALU.is_gt, fill=0.0, base=0,
                               pattern=[[1, P]], channel_multiplier=-1).then_inc(route_const, 1)

            def expert_lo(e):
                pool.wait_ge(we_hi, e + 1)
                pool.tensor_tensor(w_e[:, e, LO], we_raw[e % 2][:], w_e[:, e, HI].bitcast(F32),
                                   ALU.subtract).then_inc(we_lo, 1)

            for e in range(EXPERTS):
                expert_lo(e)

            def gather(k, r, n):
                pool.tensor_copy(id_now[:, n, :], ids[:, bass.ds(k, 1)]).then_inc(id_set, 1)
                wait_apart(pool, id_set, k + 1)
                pool.indirect_dma_start(
                    out=xg[:, n, :], out_offset=None, in_=x1_rows[:, :],
                    in_offset=bass.IndirectOffsetOnAxis(ap=id_now[:, n, :], axis=0)).then_inc(gathered[n], 16)

            def scatter(k, n):
                wait_apart(pool, out_ready, k + 1)
                pool.indirect_dma_start(
                    out=out_v, out_offset=bass.IndirectOffsetOnAxis(ap=id_now[:, n, :], axis=0),
                    in_=xg[:, n, :], in_offset=None, bounds_check=TOKENS - 1, oob_is_err=False).then_inc(scattered[n], 16)

            pool.wait_ge(ids_ready, 1)
            pool.wait_ge(zero_stored, 16)
            for j in range(TPB):
                pool.wait_ge(row_stored[j], BLOCKS * 16)
            for k in range(3):
                gather(k, 0, k)
            scatter(0, 0)
            gather(3, 0, 3)
            with pool.Fori(0, (SORTED - 7) // RING) as r:
                for n in range(RING):
                    scatter(r * RING + (n + 1), (n + 1) % RING)
                    wait_apart(pool, scattered[n], r * 16 + 16)
                    gather(r * RING + (n + 4), r + 1, n)
            for k in range(SORTED - 6, SORTED):
                scatter(k, k % RING)
                if k + 3 < SORTED:
                    pool.wait_ge(scattered[(k - 1) % RING], (k - 1) // RING * 16 + 16)
                    gather(k + 3, (k + 3) // RING, (k + 3) % RING)
            for n in range(RING):
                pool.wait_ge(scattered[n], (SORTED - n + RING - 1) // RING * 16)

        @block.vector
        def _(dve):
            def difference(n, batch=None):
                wait(dve, mixed_f32, n * 6)
                if batch is not None:
                    dve.memset(xb[:, :, 0:1], 0.0).then_inc(x_padded, 1)
                    dve.wait_ge(x_padded, batch + 1)
                dve.wait_ge(x_loaded, n * 16 + 16)
                dve.tensor_tensor(diff[:], xb[:, :, 1:], xb[:, :, 0:TB], ALU.subtract).then_inc(diffed, 1)

            def mix_matrix(n, m, first=False):
                if m == K:
                    dve.wait_ge(diffed, n + 1)
                for hp in range(2):
                    wait(dve, mixed_lo, n * 6 + (2 * m + hp - 1))
                    for c in range(2):
                        h = 2 * hp + c
                        ins = dve.scalar_tensor_tensor(out=mix[:, hp, c, :], in0=diff[:, h, :],
                                                       scalar=vec[:, VEC_MK + m, h:h + 1], in1=xb[:, h, 0:TB],
                                                       op0=ALU.mult, op1=ALU.add)
                    ins.then_inc(mixed_f32, 1)

            def enter(s):
                if not s.first:
                    dve.wait_ge(num_ready, s.g)
                src = start_state[:] if s.half == 0 else carry[:, s.p]
                if s.half == 1:
                    dve.wait_ge(carried, s.i - 1 + (s.p + 1))
                dve.tensor_copy(state[:, :, :, 0], src).then_inc(state_in, 1)

            def running_max(s):
                dve.wait_ge(state_in, s.g + 1)
                for c in range(2):
                    dve.wait_ge(proj_moved, s.g * 6 + (c + 1))
                    h = 2 * s.p + c
                    dve.tensor_tensor_scan(state[:, SQ, c, 1:], kd[:, s.p, c, :], wdec[:, h:h + 1].to_broadcast([P, TB]),
                                           state[:, SQ, c, 0:1], ALU.max, ALU.add).then_inc(maxed, 1)
                dve.wait_ge(maxed, s.g * 2 + 2)
                dve.tensor_tensor(kd[:, s.p], state[:, SQ, :, 0:TB], kd[:, s.p], ALU.subtract).then_inc(d_ready, 1)

            def clip(s):
                dve.wait_ge(d_ready, s.g + 1)
                wait(dve, a_scanned, s.g * 2)
                dve.tensor_scalar(e12[:, 0], kd[:, s.p], 0.0, None, ALU.min).then_inc(clipped, 1)
                dve.tensor_scalar(e12[:, 1], kd[:, s.p], 0.0, None, ALU.max).then_inc(clipped, 1)
                dve.wait_ge(clipped, s.g * 2 + 2)
                for c in range(2):
                    h = 2 * s.p + c
                    dve.tensor_scalar(kd[:, s.p, c, :], kd[:, s.p, c, :], uw[:, h:h + 1], -EXPONENT_CAP,
                                      ALU.subtract, ALU.max).then_inc(capped, 1)

            def result(g, p):
                dve.wait_ge(recip_guess, g + 1)
                dve.tensor_tensor(kd[:, p], kd[:, p], er[:], ALU.mult).then_inc(newton, 1)
                dve.wait_ge(newton, g * 2 + 1)
                dve.scalar_tensor_tensor(out=er[:], in0=kd[:, p], scalar=2.0, in1=er[:],
                                         op0=ALU.subtract, op1=ALU.mult).then_inc(newton, 1)
                dve.wait_ge(newton, g * 2 + 2)
                dve.scalar_tensor_tensor(out=vn[:, p], in0=vn[:, p], scalar=-1.0, in1=er[:],
                                         op0=ALU.mult, op1=ALU.mult).then_inc(wkv_done, 1)

            def scan_den(s):
                dve.wait_ge(e12_ready, s.g * 2 + 2)
                for c in range(2):
                    dve.tensor_tensor_scan(state[:, SB, c, 1:], e12[:, 0, c, :], e12[:, 1, c, :],
                                           state[:, SB, c, 0:1], ALU.mult, ALU.add).then_inc(b_scanned, 1)

            def scan_num(s):
                dve.wait_ge(ev_ready, s.g + 1)
                for c in range(2):
                    dve.tensor_tensor_scan(state[:, SA, c, 1:], e12[:, 0, c, :], e12[:, 1, c, :],
                                           state[:, SA, c, 0:1], ALU.mult, ALU.add).then_inc(a_scanned, 1)
                dve.wait_ge(big_ev, s.g + 1)
                dve.tensor_tensor(kd[:, s.p], kd[:, s.p], state[:, SB, :, 0:TB], ALU.add).then_inc(den_part, 1)
                dve.wait_ge(proj_moved, s.g * 6 + 6)
                dve.tensor_scalar(er[:], er[:], SIGMOID_CAP, None, ALU.min).then_inc(r_capped, 1)
                dve.wait_ge(r_capped, s.g + 1)
                dve.wait_ge(den_part, s.g + 1)
                dve.scalar_tensor_tensor(out=kd[:, s.p], in0=er[:], scalar=1.0, in1=kd[:, s.p],
                                         op0=ALU.add, op1=ALU.mult).then_inc(den_ready, 1)
                dve.wait_ge(a_scanned, s.g * 2 + 2)
                dve.tensor_tensor(vn[:, s.p], vn[:, s.p], state[:, SA, :, 0:TB], ALU.add).then_inc(num_ready, 1)
                if s.half == 0:
                    dve.tensor_copy(carry[:, s.p], state[:, :, :, TB]).then_inc(carried, 1)

            def add_rows(n):
                for j in range(TPB):
                    dve.wait_ge(row_loaded[j], n * 16 + 16)
                    dve.wait_ge(y_filled, n * TPB + (j + 1))
                    dve.tensor_tensor(rows[:, j], rows[:, j], y_ps[:, j % 2, :], ALU.add).then_inc(y_taken, 1)
                    if j:
                        statistics(n, j - 1)
                statistics(n, TPB - 1)
                dve.wait_ge(rstd_ready, n + 1)
                dve.scalar_tensor_tensor(out=nmr[:], in0=stats[:, :, 0], scalar=-1.0, in1=rstd[:],
                                         op0=ALU.mult, op1=ALU.mult).then_inc(nmr_ready, 1)

            def statistics(n, j):
                dve.wait_ge(y_taken, n * TPB + (j + 3))
                dve.bn_stats(bn[:, j, :], rows[:, j]).then_inc(bn_done, 1)
                wait_apart(dve, bn_done, n * TPB + (j + 1))
                dve.bn_aggr(stats[:, j, :], bn[:, j, :]).then_inc(stats_done, 1)

            def slot(s):
                mixing = s.p == 1 and s.has_next_block
                enter(s)
                running_max(s)
                clip(s)
                if mixing:
                    difference(s.i + 1, s.batch + 1 if s.half == 1 else None)
                    mix_matrix(s.i + 1, K)
                if not s.first:
                    result(s.g - 1, 1 - s.p)
                if mixing:
                    mix_matrix(s.i + 1, V)
                scan_den(s)
                if mixing:
                    mix_matrix(s.i + 1, R)
                if s.p == 0 and s.has_prev_block:
                    add_rows(s.i - 1)
                scan_num(s)

            cs = [dve.memset(zero_row[:], 0.0), dve.memset(start_state[:], 0.0),
                  dve.memset(eps_t[:], EPS), dve.memset(cap_t[:], -LN_SHIFT * LN2)]
            cs[-1].then_inc(consts_set, 1)
            dve.wait_ge(consts_set, 1)
            dve.memset(start_state[:, SQ, :], START)
            dve.wait_ge(ident_zero, 2)
            dve.tensor_scalar(part8[:], part[:], float(EXPERTS), float(EXPERTS), ALU.is_ge, ALU.mult).then_inc(vec_ready, 1)
            dve.tensor_scalar(sel_bo[:], part[0:BIAS_ROWS, 0:1].to_broadcast([BIAS_ROWS, P]), float(2 * EXPERTS), None,
                              ALU.is_ge).then_inc(sel_ready, 1)
            dve.wait_ge(vec_ready, 1)
            dve.tensor_tensor(part8[:], part[:], part8[:], ALU.subtract).then_inc(vec_ready, 1)
            dve.wait_ge(vec_ready, 2)
            dve.wait_ge(sel_ready, 1)
            dve.wait_ge(vec_loaded, 16)
            dve.tensor_scalar(nbr[:], vec[:, VEC_BR, :], -1.0, None, ALU.mult).then_inc(vec_ready, 1)
            dve.wait_ge(decay_exp, 1)
            dve.tensor_scalar(wdec[:], wdec[:], -1.0, None, ALU.mult).then_inc(vec_ready, 1)
            dve.wait_ge(vec_ready, 4)
            dve.tensor_tensor(uw[:], vec[:, VEC_FIRST, :], wdec[:], ALU.add).then_inc(vec_ready, 1)
            dve.wait_ge(vec_ready, 5)
            dve.sem_inc(y_taken, 2)
            difference(0, 0)
            for m in (K, V, R):
                mix_matrix(0, m)
            dve.wait_ge(w_lo, 4)
            walk(dve, slot, dve.Fori)
            result(SLOTS - 1, 1)
            add_rows(BLOCKS - 1)

            chain = [0]

            def link(ins):
                chain[0] += 1
                ins.then_inc(routed, 1)
                dve.wait_ge(routed, chain[0])

            def over(t, shape):
                return t.to_broadcast(shape)

            te_shape = [P, TILES, EXPERTS]
            dve.wait_ge(logits_done, TILES)
            dve.wait_ge(x1T_moved, TILES)
            for j in range(TPB):
                dve.wait_ge(row_stored[j], BLOCKS * 16)
            dve.wait_ge(route_const, 1)
            link(dve.tensor_reduce(mx[:], lg_ps[:], AX_X, ALU.max))
            hot_v, place_v = hot[:].rearrange("p e t -> p t e"), place_e[:].rearrange("p e t -> p t e")
            dve.tensor_tensor(lg[:], lg_ps[:], over(mx[:, :, None], te_shape), ALU.subtract).then_inc(shifted, 1)
            dve.wait_ge(shifted, 1)
            link(dve.tensor_scalar(place_v, lg[:], 0.0, None, ALU.is_ge))
            link(dve.tensor_tensor(place_v, place_v, over(rank8[:, None, :], te_shape), ALU.mult))
            link(dve.tensor_reduce(chosen[:], place_v, AX_X, ALU.max))
            dve.tensor_tensor(hot_v, over(chosen[:, :, None], te_shape), over(rank8[:, None, :], te_shape),
                              ALU.is_equal).then_inc(hot_ready, 1)
            dve.wait_ge(hot_ready, 1)
            dve.wait_ge(gate_exp, 1)
            link(dve.tensor_reduce(sums[:], lg[:], AX_X, ALU.add))
            link(dve.reciprocal(gate[:], sums[:]))
            flat = lambda t: t[:].rearrange("p e t -> p (e t)")
            n_te = EXPERTS * TILES
            dve.wait_ge(counted, 1)
            link(dve.tensor_tensor_scan(flat(work), flat(segment), y_ps[:, 1, 0:n_te], 0.0, ALU.mult, ALU.add))
            link(dve.tensor_tensor(place_e[:], over(work[:, :, TILES - 1:TILES], [P, EXPERTS, TILES]), steps[:], ALU.is_gt))
            link(dve.tensor_reduce(ntiles[:], place_e[:], AX_X, ALU.add))
            link(dve.tensor_tensor_scan(ends[:], over(ones[:, 0:1], [P, EXPERTS]), ntiles[:], 0.0, ALU.mult, ALU.add))
            link(dve.tensor_tensor(starts[:], ends[:], ntiles[:], ALU.subtract))
            link(dve.tensor_tensor(flat(work), flat(work), y_ps[:, 1, 0:n_te], ALU.subtract))
            link(dve.tensor_tensor(flat(work), flat(work), y_ps[:, 0, 0:n_te], ALU.add))
            link(dve.scalar_tensor_tensor(out=work[:], in0=over(starts[:, :, None], [P, EXPERTS, TILES]), scalar=float(P),
                                          in1=work[:], op0=ALU.mult, op1=ALU.add))
            link(dve.tensor_tensor(work[:], work[:], hot[:], ALU.mult))
            link(dve.tensor_reduce(dest[:], work[:].rearrange("p e t -> p t e"), AX_X, ALU.add))
            link(dve.tensor_copy(dest_i[:, 0], dest[:]))
            link(dve.tensor_scalar(dest_i[:, 1], dest_i[:, 0], 7, None, ALU.logical_shift_right))
            link(dve.tensor_scalar(dest_i[:, 2], dest_i[:, 0], P - 1, None, ALU.bitwise_and))
            link(dve.tensor_copy(dest_f[:], dest_i[:, 1:3]))
            link(dve.tensor_tensor(place_k[:, :, 1, :], over(dest_f[:, 0, :, None], [P, TILES, SORTED]),
                                   over(iota_k[:, None, :], [P, TILES, SORTED]), ALU.is_equal))
            link(dve.tensor_tensor(place_k[:, :, 0, :], place_k[:, :, 1, :], over(token1[:, :, None], [P, TILES, SORTED]), ALU.mult))
            link(dve.tensor_tensor(place_k[:, :, 1, :], place_k[:, :, 1, :], over(gate[:, :, None], [P, TILES, SORTED]), ALU.mult))
            dve.tensor_tensor(place_q[:], over(dest_f[:, 1, :, None], [P, TILES, P]), over(iota_q[:, None, :], [P, TILES, P]),
                              ALU.is_equal).then_inc(placed, 1)
            link(dve.tensor_tensor(after[:], over(iota_k[:, :, None], [P, SORTED, EXPERTS]),
                                   over(ends[:, None, :], [P, SORTED, EXPERTS]), ALU.is_ge))
            link(dve.tensor_reduce(tile_e[:], after[:], AX_X, ALU.add))
            link(dve.tensor_scalar(tile_e[:], tile_e[:], float(EXPERTS - 1), None, ALU.min))
            dve.tensor_copy(tile_ei[:], tile_e[:]).then_inc(tiles_ready, 1)
            dve.wait_ge(listed, 1)
            list_ps = t_ps[:].rearrange("p c q -> p (c q)")
            link(dve.tensor_scalar(empty[:], list_ps[:, 0:SORTED], 0.0, float(TOKENS + 1), ALU.is_equal, ALU.mult))
            link(dve.tensor_copy(gates[:], list_ps[:, SORTED:2 * SORTED]))
            dve.scalar_tensor_tensor(out=ids[:], in0=list_ps[:, 0:SORTED], scalar=-1.0, in1=empty[:],
                                     op0=ALU.add, op1=ALU.add).then_inc(ids_ready, 1)

            def turned_split_lo(k, parity):
                dve.wait_ge(turned_hi, k + 1)
                dve.tensor_tensor(xgT[:, parity, LO], t_ps[:], xgT[:, parity, HI].bitcast(F32), ALU.subtract).then_inc(turned_lo, 1)
                wait(dve, expert_filled, k - 1)
                dve.tensor_scalar(sel_e[:, parity], tile_e[0:BIAS_ROWS, bass.ds(k, 1)].to_broadcast([BIAS_ROWS, P]),
                                  part8[0:BIAS_ROWS, :], None, ALU.is_equal).then_inc(sel_set, 1)

            def add_gathered(k, n):
                dve.wait_ge(expert_filled, k + 1)
                dve.scalar_tensor_tensor(out=xg[:, n], in0=y_ps[:, n % 2, :], scalar=gates[:, bass.ds(k, 1)],
                                         in1=xg[:, n], op0=ALU.mult, op1=ALU.add).then_inc(y_taken, 1)
                dve.wait_ge(y_taken, k + (TILES + 3))
                dve.bn_stats(bn2[:, n, :], xg[:, n]).then_inc(bn2_done, 1)
                wait_apart(dve, bn2_done, k + 1)
                dve.bn_aggr(stats2[:, n, :], bn2[:, n, :]).then_inc(stats2_done, 1)

            def shift2(k, n):
                dve.wait_ge(rstd2_ready, k + 1)
                dve.scalar_tensor_tensor(out=nmr2[:, n:n + 1], in0=stats2[:, n, 0:1], scalar=-1.0, in1=rstd2[:, n:n + 1],
                                         op0=ALU.mult, op1=ALU.mult).then_inc(nmr2_ready, 1)

            turned_split_lo(0, 0)
            turned_split_lo(1, 1)
            add_gathered(0, 0)
            with dve.Fori(0, (SORTED - 3) // RING) as r:
                for n in range(RING):
                    turned_split_lo(r * RING + (n + 2), n % 2)
                    shift2(r * RING + n, n)
                    add_gathered(r * RING + (n + 1), (n + 1) % RING)
            turned_split_lo(SORTED - 1, (SORTED - 1) % 2)
            shift2(SORTED - 3, (SORTED - 3) % RING)
            add_gathered(SORTED - 2, (SORTED - 2) % RING)
            shift2(SORTED - 2, (SORTED - 2) % RING)
            add_gathered(SORTED - 1, (SORTED - 1) % RING)
            shift2(SORTED - 1, (SORTED - 1) % RING)


def kernel(**inputs):
    import numpy as np
    import concourse.bacc as bacc
    from concourse.bass_utils import run_bass_kernel_spmd

    a = {name.replace("L0_", ""): np.asarray(value) for name, value in inputs.items()}
    by_partition = lambda name: a["attn_" + name].reshape(CH, P).T
    arrays = {
        "x": a["attn_x"],
        "xT": a["attn_x"].transpose(0, 2, 1),
        "w_square": np.stack([a["attn_Wk"].T, a["attn_Wv"].T, a["attn_Wr"].T, a["attn_Wo"].T]),
        "w_experts": a["ffn_W"].transpose(0, 2, 1),
        "vectors": np.stack([by_partition(n) for n in ("bk", "bv", "br", "tmk", "tmv", "tmr", "time_decay", "time_first")], axis=1),
        "bo": a["attn_bo"].reshape(1, H),
        "b_experts": a["ffn_b"],
        "wg": a["ffn_wg"],
    }
    arrays = {name: np.ascontiguousarray(value) for name, value in arrays.items()}
    nc = bacc.Bacc("TRN2", target_bir_lowering=False, num_devices=1)
    aps = [nc.dram_tensor(name, value.shape, mybir.dt.from_np(value.dtype), kind="ExternalInput").ap()
           for name, value in arrays.items()]
    out = nc.dram_tensor("out", (BATCH, TIME, H), F32, kind="ExternalOutput").ap()
    build(nc, *aps, out)
    result = run_bass_kernel_spmd(nc, [arrays], core_ids=[0])
    return result.results[0]["out"]
```

```python
from contextlib import ExitStack

import concourse.bass as bass
from concourse import mybir

ALU = mybir.AluOpType
ACT = mybir.ActivationFunctionType
AX_X = mybir.AxisListType.X
F32 = mybir.dt.float32
F32R = mybir.dt.float32r
I32 = mybir.dt.int32
U32 = mybir.dt.uint32

P = 128
BATCH, TIME, H = 4, 1024, 512
EXPERTS = 8
CH = H // P
TB = 512
HALVES = TIME // TB
BLOCKS = BATCH * HALVES
PAIRS = CH // 2
GROUPS = BLOCKS * PAIRS
BANKS = 4
FILLS = 3 * CH
TPB = TB // P
TOKENS = BATCH * TIME
TILES = TOKENS // P
SORTED = TILES + EXPERTS - 1
RING = 6
AHEAD = 5
EPS = 1e-5
EXPONENT_CAP = 27.0
SIGMOID_CAP = 2.0 ** 80
LN_SHIFT = 60
LN2 = 0.6931471805599453
START = -1e30
K, V, R, O = range(4)
HI, LO = range(2)
EXPERT_ORDER = (0, 3, 1, 4, 2, 5, 6, 7)
SQ, SA, SB = range(3)
BIAS_ROWS = 2 * EXPERTS + 2
VEC_BK, VEC_BV, VEC_BR, VEC_MK, VEC_MV, VEC_MR, VEC_DECAY, VEC_FIRST = range(8)


def wait(eng, sem, value):
    if not isinstance(value, int) or value > 0:
        eng.wait_ge(sem, value)


class Block:

    def __init__(self, i, batch, half, first=False, last=False):
        self.i, self.batch, self.half, self.first, self.last = i, batch, half, first, last


def walk(eng, step, block_loop):
    step(Block(0, 0, 0, first=True))
    with block_loop(0, BATCH - 1) as b:
        step(Block(b * 2 + 1, b, 1))
        step(Block(b * 2 + 2, b + 1, 0))
    step(Block(BLOCKS - 1, BATCH - 1, 1, last=True))


def build(nc, x, xT, w_square, w_experts, vectors, bo, b_experts, wg, out):
    x1_rows = nc.dram_tensor("x1_rows", [TOKENS + 1, H], F32, kind="Internal").ap()

    with ExitStack() as ctx:
        cursor = [0]

        def place(name, shape, dtype, at=None):
            size = 4
            for n in shape[1:]:
                size *= n
            size = (size + 31) // 32 * 32
            offset = cursor[0] if at is None else at
            if at is None:
                cursor[0] += size
            return nc.alloc_sbuf_tensor_at(name, shape, dtype, offset=offset)

        base = nc.sbuf_base + (-nc.sbuf_base) % 32
        cursor[0] = base
        mat = 2 * CH * H * 4
        w_kvr = place("w_kvr", [P, 3, 2, CH, H], F32R)
        mixed = place("mixed", [P, 3, 2, CH, TB], F32R)
        w_o = place("w_o", [P, 2, CH, H], F32R)
        rw = place("rw", [P, 2, CH, TB], F32R)
        w_e_bytes = EXPERTS * mat
        unsplit = place("unsplit", [P, 3, 2, CH, TB], F32, at=base + 3 * mat)
        rw_unsplit = place("rw_unsplit", [P, 2, CH, TB], F32, at=base + 7 * mat)
        diff_at = cursor[0]
        diff = place("diff", [P, CH, TB], F32)
        xb_at = cursor[0]
        xb = place("xb", [P, CH, TB + 1], F32)
        temps_at = cursor[0]
        kd = place("kd", [P, 2, 2, TB], F32)
        vn = place("vn", [P, 2, 2, TB], F32)
        er = place("er", [P, 2, 2, TB], F32)
        state_at = cursor[0]
        state = place("state", [P, 3, 2, TB + 1], F32)
        e12 = place("e12", [P, 2, 2, TB], F32)
        rows_at = cursor[0]
        rows = place("rows", [P, TPB, H], F32)
        x1T = place("x1T", [P, CH, P], F32)
        bias_rows = place("bias_rows", [BIAS_ROWS, H], F32R)
        sel_bo = place("sel_bo", [BIAS_ROWS, P], F32R)
        ident = place("ident", [P, P], F32)
        vec = place("vec", [P, 8, CH], F32)
        wgs = place("wgs", [P, CH, EXPERTS], F32)
        wdec = place("wdec", [P, CH], F32)
        uw = place("uw", [P, CH], F32)
        nbr = place("nbr", [P, CH], F32)
        start_state = place("start_state", [P, 3, 2], F32)
        carry = place("carry", [P, 2, 3, 2], F32)
        bn = place("bn", [P, TPB, 6], F32)
        stats = place("stats", [P, TPB, 2], F32)
        rstd = place("rstd", [P, TPB], F32)
        nmr = place("nmr", [P, TPB], F32)
        eps_t = place("eps_t", [P, 1], F32)
        cap_t = place("cap_t", [P, 1], F32)
        part = place("part", [P, 1], F32)
        part8 = place("part8", [P, 1], F32)
        before = place("before", [P, P], F32)
        ones = place("ones", [P, P], F32)
        iota_q = place("iota_q", [P, P], F32)
        segment = place("segment", [P, EXPERTS, TILES], F32)
        steps = place("steps", [P, EXPERTS, TILES], F32)
        iota_k = place("iota_k", [P, SORTED], F32)
        token1 = place("token1", [P, TILES], F32)
        rank8 = place("rank8", [P, EXPERTS], F32)
        assert cursor[0] <= nc.sbuf_usable_end, cursor[0]
        w_raw = [place(f"w_raw{m}", [P, CH, H], F32, at=at)
                 for m, at in enumerate((temps_at, temps_at + 4 * 4 * TB, temps_at + 4 * 8 * TB, rows_at))]
        raw_at = state_at
        b_raw = place("b_raw", [EXPERTS, H], F32, at=raw_at)
        b_split = place("b_split", [EXPERTS, 2, H], F32R, at=raw_at + 4 * H)
        bo_raw = place("bo_raw", [1, H], F32, at=raw_at + 4 * 3 * H)
        bo_split = place("bo_split", [1, 2, H], F32R, at=raw_at + 4 * 4 * H)
        zero_row = place("zero_row", [1, H], F32, at=raw_at + 4 * 6 * H)
        assert raw_at + 4 * 7 * H <= rows_at
        w_e = place("w_e", [P, EXPERTS, 2, CH, H], F32R, at=base)
        assert w_e_bytes == diff_at - base
        we_raw = [place(f"we_raw{n}", [P, CH, H], F32, at=at) for n, at in enumerate((diff_at, xb_at))]
        cursor[0] = temps_at
        place_q = place("place_q", [P, TILES, P], F32)
        place_k = place("place_k", [P, TILES, 2, SORTED], F32)
        assert cursor[0] <= rows_at
        cursor[0] = temps_at
        xgT = place("xgT", [P, 3, 2, CH, P], F32R)
        xg = place("xg", [P, RING, H], F32)
        yo = place("yo", [P, RING, H], F32)
        assert cursor[0] <= rows_at
        cursor[0] = rows_at
        lg = place("lg", [P, TILES, EXPERTS], F32)
        hot = place("hot", [P, EXPERTS, TILES], F32)
        work = place("work", [P, EXPERTS, TILES], F32)
        place_e = place("place_e", [P, EXPERTS, TILES], F32)
        mx = place("mx", [P, TILES], F32)
        chosen = place("chosen", [P, TILES], F32)
        sums = place("sums", [P, TILES], F32)
        gate = place("gate", [P, TILES], F32)
        dest = place("dest", [P, TILES], F32)
        dest_i = place("dest_i", [P, 3, TILES], I32)
        dest_f = place("dest_f", [P, 2, TILES], F32)
        ntiles = place("ntiles", [P, EXPERTS], F32)
        ends = place("ends", [P, EXPERTS], F32)
        starts = place("starts", [P, EXPERTS], F32)
        after = place("after", [P, SORTED, EXPERTS], F32)
        tile_e = place("tile_e", [P, SORTED], F32)
        tile_ei = place("tile_ei", [P, SORTED], I32)
        gates = place("gates", [P, SORTED], F32)
        empty = place("empty", [P, SORTED], F32)
        ids = place("ids", [P, SORTED], U32)
        id_in = place("id_in", [P, RING, 1], U32)
        id_out = place("id_out", [P, RING, 1], U32)
        bn2 = place("bn2", [P, RING, 6], F32)
        stats2 = place("stats2", [P, RING, 2], F32)
        rstd2 = place("rstd2", [P, RING], F32)
        nmr2 = place("nmr2", [P, RING], F32)
        sel_e = place("sel_e", [BIAS_ROWS, 3, P], F32R)
        assert cursor[0] <= rows_at + 4 * (TPB * H + CH * P), cursor[0] - rows_at

        proj = ctx.enter_context(nc.psum_tensor("proj", [P, 4, TB], F32))
        y_ps = ctx.enter_context(nc.psum_tensor("y_ps", [P, 2, H], F32))
        t_ps = ctx.enter_context(nc.psum_tensor("t_ps", [P, CH, P], F32))
        lg_ps = ctx.enter_context(nc.psum_tensor("lg_ps", [P, TILES, EXPERTS], F32))

        turned_ps = [t_ps[:], proj[:, 0, :].rearrange("p (c q) -> p c q", c=CH)]

        def sem(name):
            return ctx.enter_context(nc.semaphore(name))

        waits_passed = sem("waits_passed")
        vec_loaded, w_loaded = sem("vec_loaded"), [sem(f"w_loaded{n}") for n in range(4)]
        b_loaded, wg_loaded, bias_moved, zero_stored = sem("b_loaded"), sem("wg_loaded"), sem("bias_moved"), sem("zero_stored")
        consts_set, decay_exp, vec_ready = sem("consts_set"), sem("decay_exp"), sem("vec_ready")
        w_hi, w_lo, b_hi, b_lo = sem("w_hi"), sem("w_lo"), sem("b_hi"), sem("b_lo")
        ident_zero, ident_ready, sel_ready = sem("ident_zero"), sem("ident_ready"), sem("sel_ready")
        x_loaded, x_padded, diffed, mixed_f32 = sem("x_loaded"), sem("x_padded"), sem("diffed"), sem("mixed_f32")
        mixed_hi, mixed_lo = sem("mixed_hi"), sem("mixed_lo")
        proj_filled, proj_moved = sem("proj_filled"), sem("proj_moved")
        state_in, maxed, d_ready, capped = sem("state_in"), sem("maxed"), sem("d_ready"), sem("capped")
        clipped, e12_ready, big_e = sem("clipped"), sem("e12_ready"), sem("big_e")
        b_scanned, a_scanned, carried = sem("b_scanned"), sem("a_scanned"), sem("carried")
        ev_ready, big_ev, r_capped = sem("ev_ready"), sem("big_ev"), sem("r_capped")
        num_ready, den_part, den_ready = sem("num_ready"), sem("den_part"), sem("den_ready")
        den_ln, recip_guess, newton = sem("den_ln"), sem("recip_guess"), sem("newton")
        wkv_done, rw_hi, rw_lo = sem("wkv_done"), sem("rw_hi"), sem("rw_lo")
        row_loaded = [sem(f"row_loaded{j}") for j in range(TPB)]
        row_stored = [sem(f"row_stored{j}") for j in range(TPB)]
        y_filled, y_taken, bn_done, stats_done = sem("y_filled"), sem("y_taken"), sem("bn_done"), sem("stats_done")
        row_turned, x1T_moved = sem("row_turned"), sem("x1T_moved")
        var_ln, rstd_ready, nmr_ready, x1_ready = sem("var_ln"), sem("rstd_ready"), sem("nmr_ready"), sem("x1_ready")
        logits_done = sem("logits_done")
        route_const, routed, hot_ready, shifted = sem("route_const"), sem("routed"), sem("hot_ready"), sem("shifted")
        gate_exp, counted, placed, listed = sem("gate_exp"), sem("counted"), sem("placed"), sem("listed")
        ids_ready, tiles_ready = sem("ids_ready"), sem("tiles_ready")
        we_loaded = [sem(f"we_loaded{n}") for n in range(2)]
        we_hi, we_lo = sem("we_hi"), sem("we_lo")
        id_set, id_kept, gathered = sem("id_set"), sem("id_kept"), [sem(f"gathered{n}") for n in range(RING)]
        turned, turned_hi, turned_lo, sel_set = sem("turned"), sem("turned_hi"), sem("turned_lo"), sem("sel_set")
        expert_filled, bn2_done, stats2_done = sem("expert_filled"), sem("bn2_done"), sem("stats2_done")
        var2_ln, rstd2_ready, nmr2_ready, out_ready = (
            sem("var2_ln"), sem("rstd2_ready"), sem("nmr2_ready"), sem("out_ready"))
        scattered = [sem(f"scattered{n}") for n in range(RING)]

        def wait_apart(eng, sem, value):
            if not isinstance(value, int) or value > 0:
                eng.wait_ge(sem, value)
                if not isinstance(value, int):
                    eng.sem_inc(waits_passed, 1)

        block = ctx.enter_context(nc.Block())

        xT_v = xT.rearrange("b (c p) t -> b p c t", p=P)
        x_v = x.rearrange("b (n p) h -> (b n) p h", p=P)
        x1_v = x1_rows[0:TOKENS, :].rearrange("(n p) h -> n p h", p=P)
        w_v = w_square.rearrange("m (c p) o -> m p c o", p=P)
        we_v = w_experts.rearrange("e (c p) o -> e p c o", p=P)
        out_v = out.rearrange("b t h -> (b t) h")

        @block.sync
        def _(sp):
            def load_x(n, batch, half):
                if half == 0:
                    sp.dma_start(xb[:, :, 1:], xT_v[batch, :, :, 0:TB]).then_inc(x_loaded, 16)
                else:
                    sp.dma_start(xb[:], xT_v[batch, :, :, TB - 1:]).then_inc(x_loaded, 16)

            def load_rows(n, first):
                for j in range(TPB):
                    if not first:
                        wait_apart(sp, row_turned, n * TPB + (j + 1 - TPB))
                        wait_apart(sp, row_stored[j], n * 16)
                    sp.dma_start(rows[:, j], x_v[n * TPB + j]).then_inc(row_loaded[j], 16)

            def store_rows(n):
                for j in range(TPB):
                    wait_apart(sp, x1_ready, n * TPB + (j + 1))
                    sp.dma_start(x1_v[n * TPB + j], rows[:, j]).then_inc(row_stored[j], 16)

            def load_expert(q):
                wait(sp, we_lo, q - 1)
                sp.dma_start(we_raw[q % 2][:], we_v[EXPERT_ORDER[q]]).then_inc(we_loaded[q % 2], 16)

            def step(s):
                if s.first:
                    sp.wait_ge(w_lo, 4)
                    load_rows(0, first=True)
                    return
                if not s.last:
                    wait_apart(sp, mixed_f32, s.i * 6 + 6)
                    load_x(s.i + 1, s.batch + s.half, 1 - s.half)
                else:
                    sp.wait_ge(mixed_f32, BLOCKS * 6)
                    for q in range(4):
                        load_expert(q)
                store_rows(s.i - 1)
                load_rows(s.i, first=False)

            sp.dma_start(vec[:], vectors).then_inc(vec_loaded, 16)
            load_x(0, 0, 0)
            sp.dma_start(w_raw[K][:], w_v[K]).then_inc(w_loaded[K], 16)
            sp.dma_start(b_raw[:], b_experts).then_inc(b_loaded, 16)
            sp.dma_start(bo_raw[:], bo).then_inc(b_loaded, 16)
            for n in (V, R, O):
                sp.dma_start(w_raw[n][:], w_v[n]).then_inc(w_loaded[n], 16)
            sp.dma_start(wgs[:], wg.rearrange("(c p) e -> p c e", p=P)).then_inc(wg_loaded, 16)
            sp.wait_ge(consts_set, 1)
            sp.dma_start(x1_rows[TOKENS:TOKENS + 1, :], zero_row[:]).then_inc(zero_stored, 16)
            sp.wait_ge(b_lo, 2)
            for s in range(2):
                sp.dma_start(bias_rows[s * EXPERTS:(s + 1) * EXPERTS, :].bitcast(F32), b_split[:, s, :].bitcast(F32)).then_inc(bias_moved, 16)
                sp.dma_start(bias_rows[2 * EXPERTS + s:2 * EXPERTS + s + 1, :].bitcast(F32), bo_split[:, s, :].bitcast(F32)).then_inc(bias_moved, 16)
            sp.wait_ge(mixed_f32, 6)
            load_x(1, 0, 1)
            walk(sp, step, sp.Fori)
            for q in (4, 5):
                load_expert(q)
            store_rows(BLOCKS - 1)
            for q in (6, 7):
                load_expert(q)

        @block.tensor
        def _(pe):
            def project(s, m, p, c):
                n = 4 * m + 2 * p + c
                if p == 0 and c == 0:
                    pe.wait_ge(mixed_lo, s.i * 6 + (2 * m + 2))
                    if s.first:
                        pe.wait_ge(w_lo, m + 1)
                wait(pe, proj_moved, s.i * FILLS + (n + 1 - BANKS))
                o = (2 * p + c) * P
                k = 0
                for h in range(CH):
                    for a, bb in ((HI, HI), (HI, LO), (LO, HI)):
                        mm = pe.matmul(proj[:, n % BANKS, :], w_kvr[:, m, a, h, o:o + P], mixed[:, m, bb, h, :],
                                       start=(k == 0), stop=(k == 3 * CH - 1))
                        k += 1
                mm.then_inc(proj_filled, 1)

            def project_out(n, j):
                pe.wait_ge(rw_lo, n * 2 + 2)
                if isinstance(n, int) and n == 0 and j == 0:
                    pe.wait_ge(bias_moved, 64)
                pe.wait_ge(y_taken, n * TPB + (j + 1))
                pe.matmul(y_ps[:, j % 2, :], sel_bo[:], bias_rows[:], start=True, stop=False)
                for c in range(CH):
                    for a, bb in ((HI, HI), (HI, LO), (LO, HI)):
                        mm = pe.matmul(y_ps[:, j % 2, :], rw[:, a, c, j * P:(j + 1) * P], w_o[:, bb, c, :],
                                       start=False, stop=(c == CH - 1 and (a, bb) == (LO, HI)))
                mm.then_inc(y_filled, 1)

            def turn_rows(n, j):
                pe.wait_ge(x1_ready, n * TPB + (j + 1))
                for c in range(CH):
                    mm = pe.transpose(t_ps[:, c, :], rows[:, j, c * P:(c + 1) * P], ident[:])
                mm.then_inc(row_turned, 1)

            def logits(n, j, tile):
                if isinstance(n, int) and n == 0 and j == 0:
                    pe.wait_ge(wg_loaded, 16)
                pe.wait_ge(x1T_moved, n * TPB + (j + 1))
                for c in range(CH):
                    mm = pe.matmul(lg_ps[:, tile, :], x1T[:, c, :], wgs[:, c, :], start=(c == 0), stop=(c == CH - 1))
                mm.then_inc(logits_done, 1)

            def step(s):
                for m, p in ((K, 0), (K, 1), (V, 0)):
                    project(s, m, p, 0)
                    project(s, m, p, 1)
                if not s.first:
                    for j in range(TPB):
                        project_out(s.i - 1, j)
                project(s, V, 1, 0)
                project(s, V, 1, 1)
                for j in range(TPB):
                    if not s.first:
                        turn_rows(s.i - 1, j)
                    project(s, R, j // 2, j % 2)
                    if not s.first:
                        logits(s.i - 1, j, (s.i - 1) * TPB + j)

            pe.wait_ge(sel_ready, 1)
            pe.wait_ge(ident_ready, 1)
            walk(pe, step, pe.Fori)
            last = BLOCKS - 1
            for j in range(TPB):
                project_out(last, j)
            for j in range(TPB):
                turn_rows(last, j)
                logits(last, j, last * TPB + j)

            n_te = EXPERTS * TILES
            pe.wait_ge(route_const, 1)
            pe.wait_ge(hot_ready, 1)
            hot_all = hot[:].rearrange("p e t -> p (e t)")
            pe.matmul(y_ps[:, 0, 0:n_te], before[:], hot_all, start=True, stop=True)
            pe.matmul(y_ps[:, 1, 0:n_te], ones[:], hot_all, start=True, stop=True).then_inc(counted, 1)
            pe.wait_ge(placed, 1)
            list_ps = t_ps[:].rearrange("p c q -> p (c q)")[:, 0:2 * SORTED]
            for t in range(TILES):
                mm = pe.matmul(list_ps, place_q[:, t, :], place_k[:, t].rearrange("p w k -> p (w k)"),
                               start=(t == 0), stop=(t == TILES - 1))
            mm.then_inc(listed, 1)

            def turn(k, r, n):
                pe.wait_ge(gathered[n], r * 16 + 16)
                wait(pe, turned_lo, k - 1)
                for c in range(CH):
                    mm = pe.transpose(turned_ps[n % 2][:, c, :], xg[:, n, c * P:(c + 1) * P], ident[:])
                mm.then_inc(turned, 1)

            def expert(k, n):
                parity, third = n % 2, n % 3
                e = pe.value_load(tile_ei[0:1, bass.ds(k, 1)], min_val=0, max_val=EXPERTS - 1)
                pe.wait_ge(turned_lo, k + 1)
                pe.wait_ge(sel_set, k + 1)
                pe.wait_ge(y_taken, k + (TILES + 1))
                pe.matmul(y_ps[:, parity, :], sel_e[:, third, :], bias_rows[:], start=True, stop=False)
                for c in range(CH):
                    for a, bb in ((HI, HI), (HI, LO), (LO, HI)):
                        mm = pe.matmul(y_ps[:, parity, :], xgT[:, third, a, c, :],
                                       w_e[:, bass.ds(e, 1), bb, c, :].rearrange("p u o -> p (u o)"),
                                       start=False, stop=(c == CH - 1 and (a, bb) == (LO, HI)))
                mm.then_inc(expert_filled, 1)

            pe.wait_ge(tiles_ready, 1)
            pe.wait_ge(ids_ready, 1)
            pe.wait_ge(we_lo, EXPERTS)
            turn(0, 0, 0)
            turn(1, 0, 1)
            with pe.Fori(0, SORTED // RING) as r:
                for n in range(RING):
                    turn(r * RING + (n + 2), r + (n + 2) // RING, (n + 2) % RING)
                    expert(r * RING + n, n)
            for k in range(SORTED // RING * RING, SORTED):
                if k + 2 < SORTED:
                    turn(k + 2, (k + 2) // RING, (k + 2) % RING)
                expert(k, k % RING)

        @block.scalar
        def _(act):
            def mix_hi(n, m):
                for hp in range(2):
                    act.wait_ge(mixed_f32, n * 6 + (2 * m + hp + 1))
                    act.activation(mixed[:, m, HI, 2 * hp:2 * hp + 2, :], unsplit[:, m, LO, 2 * hp:2 * hp + 2, :],
                                   ACT.Copy).then_inc(mixed_hi, 1)

            def evacuate(s, m, p, c):
                n = 4 * m + 2 * p + c
                bank = proj[:, n % BANKS, :]
                act.wait_ge(proj_filled, s.i * FILLS + (n + 1))
                if not s.first:
                    act.wait_ge(wkv_done, s.i * 2 + (p - 1))
                col = slice(2 * p + c, 2 * p + c + 1)
                if m == K:
                    ins = act.activation(kd[:, p, c, :], bank, ACT.Identity, bias=vec[:, VEC_BK, col])
                elif m == V:
                    ins = act.activation(vn[:, p, c, :], bank, ACT.Identity, bias=vec[:, VEC_BV, col])
                else:
                    ins = act.activation(er[:, p, c, :], bank, ACT.Exp, bias=nbr[:, col], scale=-1.0)
                ins.then_inc(proj_moved, 1)

            def exponentials(s, p):
                g = s.i * 2 + p
                act.wait_ge(clipped, g * 2 + 1)
                act.activation(e12[:, 0], e12[:, 0], ACT.Exp).then_inc(e12_ready, 1)
                act.wait_ge(clipped, g * 2 + 2)
                act.activation(e12[:, 1], e12[:, 1], ACT.Exp, scale=-1.0).then_inc(e12_ready, 1)
                act.wait_ge(capped, g * 2 + 2)
                act.activation(kd[:, p], kd[:, p], ACT.Exp, scale=-1.0).then_inc(big_e, 1)

            def rwkv_hi(i, p):
                act.wait_ge(wkv_done, i * 2 + (p + 1))
                act.activation(rw[:, HI, 2 * p:2 * p + 2, :], rw_unsplit[:, LO, 2 * p:2 * p + 2, :], ACT.Copy).then_inc(rw_hi, 1)

            def reciprocal_guess(i, p):
                g = i * 2 + p
                act.wait_ge(den_ready, g + 1)
                act.activation(er[:, p], kd[:, p], ACT.Ln, scale=2.0 ** -LN_SHIFT).then_inc(den_ln, 1)
                act.wait_ge(den_ln, g + 1)
                act.activation(er[:, p], er[:, p], ACT.Exp, bias=cap_t[:], scale=-1.0).then_inc(recip_guess, 1)

            def norm(n):
                act.wait_ge(stats_done, n * TPB + TPB)
                act.activation(rstd[:], stats[:, :, 1], ACT.Ln, bias=eps_t[:]).then_inc(var_ln, 1)
                act.wait_ge(var_ln, n + 1)
                act.activation(rstd[:], rstd[:], ACT.Exp, scale=-0.5).then_inc(rstd_ready, 1)
                act.wait_ge(nmr_ready, n + 1)
                for j in range(TPB):
                    act.activation(rows[:, j], rows[:, j], ACT.Identity, bias=nmr[:, j:j + 1],
                                   scale=rstd[:, j:j + 1]).then_inc(x1_ready, 1)

            def move_turned(n, j):
                act.wait_ge(row_turned, n * TPB + (j + 1))
                act.activation(x1T[:], t_ps[:], ACT.Copy).then_inc(x1T_moved, 1)

            def expert_hi(q):
                e = EXPERT_ORDER[q]
                act.wait_ge(we_loaded[q % 2], q // 2 * 16 + 16)
                act.activation(w_e[:, e, HI], we_raw[q % 2][:], ACT.Copy).then_inc(we_hi, 1)

            def step(s):
                turning = not s.first
                if not s.first:
                    reciprocal_guess(s.i - 1, 1)
                    mix_hi(s.i, R)
                evacuate(s, K, 0, 0)
                evacuate(s, K, 0, 1)
                if not s.first:
                    rwkv_hi(s.i - 1, 1)
                evacuate(s, K, 1, 0)
                evacuate(s, K, 1, 1)
                exponentials(s, 0)
                evacuate(s, V, 0, 0)
                evacuate(s, V, 0, 1)
                if s.last:
                    expert_hi(0)
                    expert_hi(1)
                else:
                    mix_hi(s.i + 1, K)
                exponentials(s, 1)
                evacuate(s, V, 1, 0)
                evacuate(s, V, 1, 1)
                if not s.first:
                    norm(s.i - 1)
                    move_turned(s.i - 1, 0)
                evacuate(s, R, 0, 0)
                if s.last:
                    expert_hi(2)
                else:
                    mix_hi(s.i + 1, V)
                if turning:
                    move_turned(s.i - 1, 1)
                evacuate(s, R, 0, 1)
                if turning:
                    move_turned(s.i - 1, 2)
                evacuate(s, R, 1, 0)
                reciprocal_guess(s.i, 0)
                if turning:
                    move_turned(s.i - 1, 3)
                evacuate(s, R, 1, 1)
                rwkv_hi(s.i, 0)

            act.preload_act_table_set("natural_log_exp_and_others")
            act.wait_ge(vec_loaded, 16)
            act.activation(wdec[:], vec[:, VEC_DECAY, :], ACT.Exp).then_inc(decay_exp, 1)
            act.wait_ge(w_loaded[K], 16)
            act.activation(w_kvr[:, K, HI], w_raw[K][:], ACT.Copy).then_inc(w_hi, 1)
            mix_hi(0, K)
            act.wait_ge(b_loaded, 32)
            act.activation(b_split[:, HI], b_raw[:], ACT.Copy).then_inc(b_hi, 1)
            act.activation(bo_split[:, HI], bo_raw[:], ACT.Copy).then_inc(b_hi, 1)
            for m in (V, R, O):
                act.wait_ge(w_loaded[m], 16)
                dst = w_o[:, HI] if m == O else w_kvr[:, m, HI]
                act.activation(dst, w_raw[m][:], ACT.Copy).then_inc(w_hi, 1)
                if m != O:
                    mix_hi(0, m)
            act.wait_ge(consts_set, 1)
            act.wait_ge(w_lo, 3)
            walk(act, step, act.Fori)
            last = BLOCKS - 1
            reciprocal_guess(last, 1)
            rwkv_hi(last, 1)
            for q in range(3, 6):
                expert_hi(q)
            norm(last)
            for j in range(TPB):
                move_turned(last, j)
            act.wait_ge(y_filled, TILES)
            expert_hi(6)
            expert_hi(7)
            act.wait_ge(hot_ready, 1)
            act.activation(lg[:], lg[:], ACT.Exp).then_inc(gate_exp, 1)

            def turned_split_hi(k, n):
                act.wait_ge(turned, k + 1)
                wait(act, expert_filled, k - 2)
                act.activation(xgT[:, n % 3, HI], turned_ps[n % 2], ACT.Copy).then_inc(turned_hi, 1)

            def norm2(k, n):
                act.wait_ge(stats2_done, k + 1)
                act.activation(rstd2[:, n:n + 1], stats2[:, n, 1:2], ACT.Ln, bias=eps_t[:]).then_inc(var2_ln, 1)
                act.wait_ge(var2_ln, k + 1)
                act.activation(rstd2[:, n:n + 1], rstd2[:, n:n + 1], ACT.Exp, scale=-0.5).then_inc(rstd2_ready, 1)
                act.wait_ge(nmr2_ready, k + 1)
                act.activation(yo[:, n], yo[:, n], ACT.Identity, bias=nmr2[:, n:n + 1],
                               scale=rstd2[:, n:n + 1]).then_inc(out_ready, 1)

            act.wait_ge(listed, 1)
            for k in range(3):
                turned_split_hi(k, k)
            rounds = (SORTED - 3) // RING
            with act.Fori(0, rounds) as r:
                for n in range(RING):
                    turned_split_hi(r * RING + (n + 3), (n + 3) % RING)
                    norm2(r * RING + n, n)
            for k in range(rounds * RING, SORTED):
                if k + 3 < SORTED:
                    turned_split_hi(k + 3, (k + 3) % RING)
                norm2(k, k % RING)

        @block.gpsimd
        def _(pool):
            def mix_lo(n, m):
                for hp in range(2):
                    pool.wait_ge(mixed_hi, n * 6 + (2 * m + hp + 1))
                    pool.tensor_tensor(mixed[:, m, LO, 2 * hp:2 * hp + 2, :], unsplit[:, m, LO, 2 * hp:2 * hp + 2, :],
                                       mixed[:, m, HI, 2 * hp:2 * hp + 2, :].bitcast(F32),
                                       ALU.subtract).then_inc(mixed_lo, 1)

            def rwkv_lo(i, p):
                pool.wait_ge(rw_hi, i * 2 + (p + 1))
                pool.tensor_tensor(rw[:, LO, 2 * p:2 * p + 2, :], rw_unsplit[:, LO, 2 * p:2 * p + 2, :],
                                   rw[:, HI, 2 * p:2 * p + 2, :].bitcast(F32), ALU.subtract).then_inc(rw_lo, 1)

            def weigh_v(s, p):
                g = s.i * 2 + p
                pool.wait_ge(b_scanned, g * 2 + 2)
                pool.wait_ge(proj_moved, s.i * FILLS + (4 * V + 2 * p + 2))
                pool.tensor_tensor(e12[:, 1], e12[:, 1], vn[:, p], ALU.mult).then_inc(ev_ready, 1)
                pool.wait_ge(big_e, g + 1)
                pool.wait_ge(ev_ready, g + 1)
                pool.tensor_tensor(vn[:, p], vn[:, p], kd[:, p], ALU.mult).then_inc(big_ev, 1)

            def expert_lo(q):
                e = EXPERT_ORDER[q]
                pool.wait_ge(we_hi, q + 1)
                pool.tensor_tensor(w_e[:, e, LO], we_raw[q % 2][:], w_e[:, e, HI].bitcast(F32),
                                   ALU.subtract).then_inc(we_lo, 1)

            def step(s):
                if not s.first:
                    rwkv_lo(s.i - 1, 1)
                    mix_lo(s.i, R)
                weigh_v(s, 0)
                if s.last:
                    expert_lo(0)
                    expert_lo(1)
                else:
                    mix_lo(s.i + 1, K)
                weigh_v(s, 1)
                if s.last:
                    expert_lo(2)
                else:
                    mix_lo(s.i + 1, V)
                rwkv_lo(s.i, 0)

            pool.memset(ident[:], 0.0).then_inc(ident_zero, 1)
            pool.wait_ge(ident_zero, 1)
            pool.affine_select(out=ident[:], in_=ident[:], compare_op=ALU.not_equal, fill=1.0, base=0,
                               pattern=[[-1, P]], channel_multiplier=1).then_inc(ident_ready, 1)
            pool.iota(part[:], pattern=[[0, 1]], base=0, channel_multiplier=1,
                      allow_small_or_imprecise_dtypes=True).then_inc(ident_zero, 1)
            rc = []
            rc.append(pool.memset(before[:], 1.0))
            rc.append(pool.memset(ones[:], 1.0))
            rc.append(pool.memset(segment[:], 1.0))
            rc.append(pool.iota(iota_q[:], pattern=[[1, P]], base=0, channel_multiplier=0, allow_small_or_imprecise_dtypes=True))
            rc.append(pool.iota(steps[:], pattern=[[0, EXPERTS], [P, TILES]], base=0, channel_multiplier=0, allow_small_or_imprecise_dtypes=True))
            rc.append(pool.iota(iota_k[:], pattern=[[1, SORTED]], base=0, channel_multiplier=0, allow_small_or_imprecise_dtypes=True))
            rc.append(pool.iota(token1[:], pattern=[[P, TILES]], base=1, channel_multiplier=1, allow_small_or_imprecise_dtypes=True))
            rc.append(pool.iota(rank8[:], pattern=[[-1, EXPERTS]], base=EXPERTS, channel_multiplier=0, allow_small_or_imprecise_dtypes=True))
            rc[-1].then_inc(ident_zero, 1)
            pool.wait_ge(ident_zero, 3)
            pool.memset(segment[:, :, 0:1], 0.0)
            pool.affine_select(out=before[:], in_=before[:], compare_op=ALU.is_gt, fill=0.0, base=0,
                               pattern=[[1, P]], channel_multiplier=-1).then_inc(route_const, 1)
            for m in (K, V, R, O):
                pool.wait_ge(w_hi, m + 1)
                hi, lo = (w_o[:, HI], w_o[:, LO]) if m == O else (w_kvr[:, m, HI], w_kvr[:, m, LO])
                pool.tensor_tensor(lo, w_raw[m][:], hi.bitcast(F32), ALU.subtract).then_inc(w_lo, 1)
                if m in (V, R):
                    mix_lo(0, m)
            walk(pool, step, pool.Fori)
            rwkv_lo(BLOCKS - 1, 1)
            for q in range(3, EXPERTS):
                expert_lo(q)

            def gather(k, r, n):
                pool.tensor_copy(id_in[:, n, :], ids[:, bass.ds(k, 1)]).then_inc(id_set, 1)
                wait_apart(pool, id_set, k + 1)
                pool.indirect_dma_start(
                    out=xg[:, n, :], out_offset=None, in_=x1_rows[:, :],
                    in_offset=bass.IndirectOffsetOnAxis(ap=id_in[:, n, :], axis=0)).then_inc(gathered[n], 16)

            def scatter(k, n):
                wait_apart(pool, out_ready, k + 1)
                pool.tensor_copy(id_out[:, n, :], id_in[:, n, :]).then_inc(id_kept, 1)
                wait_apart(pool, id_kept, k + 1)
                pool.indirect_dma_start(
                    out=out_v, out_offset=bass.IndirectOffsetOnAxis(ap=id_out[:, n, :], axis=0),
                    in_=yo[:, n, :], in_offset=None, bounds_check=TOKENS - 1, oob_is_err=False).then_inc(scattered[n], 16)

            pool.wait_ge(ids_ready, 1)
            pool.wait_ge(zero_stored, 16)
            for j in range(TPB):
                pool.wait_ge(row_stored[j], BLOCKS * 16)
            for k in range(AHEAD):
                gather(k, 0, k)
            rounds = (SORTED - AHEAD) // RING
            with pool.Fori(0, rounds) as r:
                for n in range(RING):
                    ahead = AHEAD + n
                    pool.wait_ge(y_taken, r * RING + (TILES + n + AHEAD - RING + 3))
                    gather(r * RING + ahead, r + ahead // RING, ahead % RING)
                    scatter(r * RING + n, n)
            for k in range(rounds * RING, SORTED):
                if k + AHEAD < SORTED:
                    pool.wait_ge(y_taken, TILES + k + AHEAD - RING + 3)
                    gather(k + AHEAD, (k + AHEAD) // RING, (k + AHEAD) % RING)
                scatter(k, k % RING)
            for n in range(RING):
                pool.wait_ge(scattered[n], (SORTED - n + RING - 1) // RING * 16)

        @block.vector
        def _(dve):
            def difference(n, batch=None):
                wait(dve, mixed_f32, n * 6)
                if batch is not None:
                    dve.memset(xb[:, :, 0:1], 0.0).then_inc(x_padded, 1)
                    dve.wait_ge(x_padded, batch + 1)
                dve.wait_ge(x_loaded, n * 16 + 16)
                dve.tensor_tensor(diff[:], xb[:, :, 1:], xb[:, :, 0:TB], ALU.subtract).then_inc(diffed, 1)

            def mix_matrix(n, m):
                dve.wait_ge(diffed, n + 1)
                wait(dve, proj_filled, n * FILLS + (4 * m + 4 - FILLS))
                for hp in range(2):
                    for c in range(2):
                        h = 2 * hp + c
                        ins = dve.scalar_tensor_tensor(out=unsplit[:, m, LO, h, :], in0=diff[:, h, :],
                                                       scalar=vec[:, VEC_MK + m, h:h + 1], in1=xb[:, h, 0:TB],
                                                       op0=ALU.mult, op1=ALU.add)
                    ins.then_inc(mixed_f32, 1)

            def running_max(s, p):
                g = s.i * 2 + p
                wait(dve, num_ready, g)
                src = start_state[:] if s.half == 0 else carry[:, p]
                if s.half == 1:
                    dve.wait_ge(carried, s.i - 1 + (p + 1))
                dve.tensor_copy(state[:, :, :, 0], src).then_inc(state_in, 1)
                dve.wait_ge(state_in, g + 1)
                for c in range(2):
                    dve.wait_ge(proj_moved, s.i * FILLS + (4 * K + 2 * p + c + 1))
                    h = 2 * p + c
                    dve.tensor_tensor_scan(state[:, SQ, c, 1:], kd[:, p, c, :], wdec[:, h:h + 1].to_broadcast([P, TB]),
                                           state[:, SQ, c, 0:1], ALU.max, ALU.add).then_inc(maxed, 1)
                dve.wait_ge(maxed, g * 2 + 2)
                dve.tensor_tensor(kd[:, p], state[:, SQ, :, 0:TB], kd[:, p], ALU.subtract).then_inc(d_ready, 1)
                dve.wait_ge(d_ready, g + 1)
                wait(dve, a_scanned, g * 2)
                dve.tensor_scalar(e12[:, 0], kd[:, p], 0.0, None, ALU.min).then_inc(clipped, 1)
                dve.tensor_scalar(e12[:, 1], kd[:, p], 0.0, None, ALU.max).then_inc(clipped, 1)
                dve.wait_ge(clipped, g * 2 + 2)
                for c in range(2):
                    h = 2 * p + c
                    dve.tensor_scalar(kd[:, p, c, :], kd[:, p, c, :], uw[:, h:h + 1], -EXPONENT_CAP,
                                      ALU.subtract, ALU.max).then_inc(capped, 1)

            def scan_den(s, p):
                g = s.i * 2 + p
                dve.wait_ge(e12_ready, g * 2 + 2)
                for c in range(2):
                    dve.tensor_tensor_scan(state[:, SB, c, 1:], e12[:, 0, c, :], e12[:, 1, c, :],
                                           state[:, SB, c, 0:1], ALU.mult, ALU.add).then_inc(b_scanned, 1)

            def scan_num(s, p):
                g = s.i * 2 + p
                dve.wait_ge(ev_ready, g + 1)
                for c in range(2):
                    dve.tensor_tensor_scan(state[:, SA, c, 1:], e12[:, 0, c, :], e12[:, 1, c, :],
                                           state[:, SA, c, 0:1], ALU.mult, ALU.add).then_inc(a_scanned, 1)
                dve.wait_ge(big_ev, g + 1)
                dve.tensor_tensor(kd[:, p], kd[:, p], state[:, SB, :, 0:TB], ALU.add).then_inc(den_part, 1)
                dve.wait_ge(a_scanned, g * 2 + 2)
                dve.tensor_tensor(vn[:, p], vn[:, p], state[:, SA, :, 0:TB], ALU.add).then_inc(num_ready, 1)
                if s.half == 0:
                    dve.tensor_copy(carry[:, p], state[:, :, :, TB]).then_inc(carried, 1)

            def denominator(i, p):
                g = i * 2 + p
                dve.wait_ge(proj_moved, i * FILLS + (4 * R + 2 * p + 2))
                dve.tensor_scalar(er[:, p], er[:, p], SIGMOID_CAP, None, ALU.min).then_inc(r_capped, 1)
                dve.wait_ge(r_capped, g + 1)
                dve.wait_ge(den_part, g + 1)
                dve.scalar_tensor_tensor(out=kd[:, p], in0=er[:, p], scalar=1.0, in1=kd[:, p],
                                         op0=ALU.add, op1=ALU.mult).then_inc(den_ready, 1)

            def result(i, p):
                g = i * 2 + p
                dve.wait_ge(recip_guess, g + 1)
                dve.tensor_tensor(kd[:, p], kd[:, p], er[:, p], ALU.mult).then_inc(newton, 1)
                dve.wait_ge(newton, g * 2 + 1)
                dve.scalar_tensor_tensor(out=er[:, p], in0=kd[:, p], scalar=2.0, in1=er[:, p],
                                         op0=ALU.subtract, op1=ALU.mult).then_inc(newton, 1)
                dve.wait_ge(newton, g * 2 + 2)
                wait(dve, y_filled, i * TPB)
                dve.wait_ge(num_ready, g + 1)
                dve.scalar_tensor_tensor(out=rw_unsplit[:, LO, 2 * p:2 * p + 2, :], in0=vn[:, p], scalar=-1.0,
                                         in1=er[:, p], op0=ALU.mult, op1=ALU.mult).then_inc(wkv_done, 1)

            def add_rows(n, j):
                dve.wait_ge(row_loaded[j], n * 16 + 16)
                dve.wait_ge(y_filled, n * TPB + (j + 1))
                dve.tensor_tensor(rows[:, j], rows[:, j], y_ps[:, j % 2, :], ALU.add).then_inc(y_taken, 1)

            def shift(n):
                dve.wait_ge(rstd_ready, n + 1)
                dve.scalar_tensor_tensor(out=nmr[:], in0=stats[:, :, 0], scalar=-1.0, in1=rstd[:],
                                         op0=ALU.mult, op1=ALU.mult).then_inc(nmr_ready, 1)

            def statistics(n, j):
                dve.wait_ge(y_taken, n * TPB + (j + 3))
                dve.bn_stats(bn[:, j, :], rows[:, j]).then_inc(bn_done, 1)
                wait_apart(dve, bn_done, n * TPB + (j + 1))
                dve.bn_aggr(stats[:, j, :], bn[:, j, :]).then_inc(stats_done, 1)

            def step(s):
                if not s.first:
                    mix_matrix(s.i, R)
                    result(s.i - 1, 1)
                running_max(s, 0)
                if not s.last:
                    difference(s.i + 1, s.batch + 1 if s.half == 1 else None)
                scan_den(s, 0)
                if not s.last:
                    mix_matrix(s.i + 1, K)
                if not s.first:
                    add_rows(s.i - 1, 0)
                scan_num(s, 0)
                if not s.first:
                    add_rows(s.i - 1, 1)
                    statistics(s.i - 1, 0)
                running_max(s, 1)
                if not s.first:
                    add_rows(s.i - 1, 2)
                    statistics(s.i - 1, 1)
                    add_rows(s.i - 1, 3)
                    statistics(s.i - 1, 2)
                    statistics(s.i - 1, 3)
                scan_den(s, 1)
                if not s.first:
                    shift(s.i - 1)
                if not s.last:
                    mix_matrix(s.i + 1, V)
                scan_num(s, 1)
                denominator(s.i, 0)
                denominator(s.i, 1)
                result(s.i, 0)

            cs = [dve.memset(zero_row[:], 0.0), dve.memset(start_state[:], 0.0),
                  dve.memset(eps_t[:], EPS), dve.memset(cap_t[:], -LN_SHIFT * LN2)]
            cs[-1].then_inc(consts_set, 1)
            dve.wait_ge(consts_set, 1)
            dve.memset(start_state[:, SQ, :], START)
            dve.wait_ge(ident_zero, 2)
            dve.tensor_scalar(part8[:], part[:], float(EXPERTS), float(EXPERTS), ALU.is_ge, ALU.mult).then_inc(vec_ready, 1)
            dve.tensor_scalar(sel_bo[:], part[0:BIAS_ROWS, 0:1].to_broadcast([BIAS_ROWS, P]), float(2 * EXPERTS), None,
                              ALU.is_ge).then_inc(sel_ready, 1)
            dve.wait_ge(vec_ready, 1)
            dve.tensor_tensor(part8[:], part[:], part8[:], ALU.subtract).then_inc(vec_ready, 1)
            dve.wait_ge(vec_ready, 2)
            dve.wait_ge(sel_ready, 1)
            dve.wait_ge(vec_loaded, 16)
            dve.tensor_scalar(nbr[:], vec[:, VEC_BR, :], -1.0, None, ALU.mult).then_inc(vec_ready, 1)
            dve.wait_ge(decay_exp, 1)
            dve.tensor_scalar(wdec[:], wdec[:], -1.0, None, ALU.mult).then_inc(vec_ready, 1)
            dve.wait_ge(vec_ready, 4)
            dve.tensor_tensor(uw[:], vec[:, VEC_FIRST, :], wdec[:], ALU.add).then_inc(vec_ready, 1)
            dve.wait_ge(vec_ready, 5)
            dve.sem_inc(y_taken, 2)
            difference(0, 0)
            mix_matrix(0, K)
            for hp in range(2):
                dve.wait_ge(mixed_hi, hp + 1)
                dve.tensor_tensor(mixed[:, K, LO, 2 * hp:2 * hp + 2, :], unsplit[:, K, LO, 2 * hp:2 * hp + 2, :],
                                  mixed[:, K, HI, 2 * hp:2 * hp + 2, :].bitcast(F32),
                                  ALU.subtract).then_inc(mixed_lo, 1)
            mix_matrix(0, V)
            mix_matrix(0, R)
            dve.wait_ge(b_hi, 2)
            dve.tensor_tensor(b_split[:, LO], b_raw[:], b_split[:, HI].bitcast(F32), ALU.subtract).then_inc(b_lo, 1)
            dve.tensor_tensor(bo_split[:, LO], bo_raw[:], bo_split[:, HI].bitcast(F32), ALU.subtract).then_inc(b_lo, 1)
            dve.wait_ge(bias_moved, 64)
            dve.wait_ge(zero_stored, 16)
            walk(dve, step, dve.Fori)
            last = BLOCKS - 1
            result(last, 1)
            for j in range(TPB):
                add_rows(last, j)
                if j:
                    statistics(last, j - 1)
            statistics(last, TPB - 1)
            shift(last)

            chain = [0]

            def link(ins):
                chain[0] += 1
                ins.then_inc(routed, 1)
                dve.wait_ge(routed, chain[0])

            def over(t, shape):
                return t.to_broadcast(shape)

            te_shape = [P, TILES, EXPERTS]
            dve.wait_ge(logits_done, TILES)
            dve.wait_ge(x1T_moved, TILES)
            for j in range(TPB):
                dve.wait_ge(row_stored[j], BLOCKS * 16)
            dve.wait_ge(route_const, 1)
            link(dve.tensor_reduce(mx[:], lg_ps[:], AX_X, ALU.max))
            hot_v, place_v = hot[:].rearrange("p e t -> p t e"), place_e[:].rearrange("p e t -> p t e")
            dve.tensor_tensor(lg[:], lg_ps[:], over(mx[:, :, None], te_shape), ALU.subtract).then_inc(shifted, 1)
            dve.wait_ge(shifted, 1)
            link(dve.tensor_scalar(place_v, lg[:], 0.0, None, ALU.is_ge))
            link(dve.tensor_tensor(place_v, place_v, over(rank8[:, None, :], te_shape), ALU.mult))
            link(dve.tensor_reduce(chosen[:], place_v, AX_X, ALU.max))
            dve.tensor_tensor(hot_v, over(chosen[:, :, None], te_shape), over(rank8[:, None, :], te_shape),
                              ALU.is_equal).then_inc(hot_ready, 1)
            dve.wait_ge(hot_ready, 1)
            dve.wait_ge(gate_exp, 1)
            link(dve.tensor_reduce(sums[:], lg[:], AX_X, ALU.add))
            link(dve.reciprocal(gate[:], sums[:]))
            flat = lambda t: t[:].rearrange("p e t -> p (e t)")
            n_te = EXPERTS * TILES
            dve.wait_ge(counted, 1)
            link(dve.tensor_tensor_scan(flat(work), flat(segment), y_ps[:, 1, 0:n_te], 0.0, ALU.mult, ALU.add))
            link(dve.tensor_tensor(place_e[:], over(work[:, :, TILES - 1:TILES], [P, EXPERTS, TILES]), steps[:], ALU.is_gt))
            link(dve.tensor_reduce(ntiles[:], place_e[:], AX_X, ALU.add))
            link(dve.tensor_tensor_scan(ends[:], over(ones[:, 0:1], [P, EXPERTS]), ntiles[:], 0.0, ALU.mult, ALU.add))
            link(dve.tensor_tensor(starts[:], ends[:], ntiles[:], ALU.subtract))
            link(dve.tensor_tensor(flat(work), flat(work), y_ps[:, 1, 0:n_te], ALU.subtract))
            link(dve.tensor_tensor(flat(work), flat(work), y_ps[:, 0, 0:n_te], ALU.add))
            link(dve.scalar_tensor_tensor(out=work[:], in0=over(starts[:, :, None], [P, EXPERTS, TILES]), scalar=float(P),
                                          in1=work[:], op0=ALU.mult, op1=ALU.add))
            link(dve.tensor_tensor(work[:], work[:], hot[:], ALU.mult))
            link(dve.tensor_reduce(dest[:], work[:].rearrange("p e t -> p t e"), AX_X, ALU.add))
            link(dve.tensor_copy(dest_i[:, 0], dest[:]))
            link(dve.tensor_scalar(dest_i[:, 1], dest_i[:, 0], 7, None, ALU.logical_shift_right))
            link(dve.tensor_scalar(dest_i[:, 2], dest_i[:, 0], P - 1, None, ALU.bitwise_and))
            link(dve.tensor_copy(dest_f[:], dest_i[:, 1:3]))
            link(dve.tensor_tensor(place_k[:, :, 1, :], over(dest_f[:, 0, :, None], [P, TILES, SORTED]),
                                   over(iota_k[:, None, :], [P, TILES, SORTED]), ALU.is_equal))
            link(dve.tensor_tensor(place_k[:, :, 0, :], place_k[:, :, 1, :], over(token1[:, :, None], [P, TILES, SORTED]), ALU.mult))
            link(dve.tensor_tensor(place_k[:, :, 1, :], place_k[:, :, 1, :], over(gate[:, :, None], [P, TILES, SORTED]), ALU.mult))
            dve.tensor_tensor(place_q[:], over(dest_f[:, 1, :, None], [P, TILES, P]), over(iota_q[:, None, :], [P, TILES, P]),
                              ALU.is_equal).then_inc(placed, 1)
            link(dve.tensor_tensor(after[:], over(iota_k[:, :, None], [P, SORTED, EXPERTS]),
                                   over(ends[:, None, :], [P, SORTED, EXPERTS]), ALU.is_ge))
            link(dve.tensor_reduce(tile_e[:], after[:], AX_X, ALU.add))
            link(dve.tensor_scalar(tile_e[:], tile_e[:], float(EXPERTS - 1), None, ALU.min))
            dve.tensor_copy(tile_ei[:], tile_e[:]).then_inc(tiles_ready, 1)
            dve.wait_ge(listed, 1)
            list_ps = t_ps[:].rearrange("p c q -> p (c q)")
            link(dve.tensor_scalar(empty[:], list_ps[:, 0:SORTED], 0.0, float(TOKENS + 1), ALU.is_equal, ALU.mult))
            link(dve.tensor_copy(gates[:], list_ps[:, SORTED:2 * SORTED]))
            dve.scalar_tensor_tensor(out=ids[:], in0=list_ps[:, 0:SORTED], scalar=-1.0, in1=empty[:],
                                     op0=ALU.add, op1=ALU.add).then_inc(ids_ready, 1)

            def turned_split_lo(k, n):
                dve.wait_ge(turned_hi, k + 1)
                dve.tensor_tensor(xgT[:, n % 3, LO], turned_ps[n % 2], xgT[:, n % 3, HI].bitcast(F32), ALU.subtract).then_inc(turned_lo, 1)
                wait(dve, expert_filled, k - 2)
                dve.tensor_scalar(sel_e[:, n % 3], tile_e[0:BIAS_ROWS, bass.ds(k, 1)].to_broadcast([BIAS_ROWS, P]),
                                  part8[0:BIAS_ROWS, :], None, ALU.is_equal).then_inc(sel_set, 1)

            def add_gathered(k, r, n):
                dve.wait_ge(expert_filled, k + 1)
                wait(dve, scattered[n], r * 16)
                dve.scalar_tensor_tensor(out=yo[:, n], in0=y_ps[:, n % 2, :], scalar=gates[:, bass.ds(k, 1)],
                                         in1=xg[:, n], op0=ALU.mult, op1=ALU.add).then_inc(y_taken, 1)
                dve.wait_ge(y_taken, k + (TILES + 3))
                dve.bn_stats(bn2[:, n, :], yo[:, n]).then_inc(bn2_done, 1)
                wait_apart(dve, bn2_done, k + 1)
                dve.bn_aggr(stats2[:, n, :], bn2[:, n, :]).then_inc(stats2_done, 1)

            def shift2(k, n):
                dve.wait_ge(rstd2_ready, k + 1)
                dve.scalar_tensor_tensor(out=nmr2[:, n:n + 1], in0=stats2[:, n, 0:1], scalar=-1.0, in1=rstd2[:, n:n + 1],
                                         op0=ALU.mult, op1=ALU.mult).then_inc(nmr2_ready, 1)

            for k in range(3):
                turned_split_lo(k, k)
            add_gathered(0, 0, 0)
            rounds = (SORTED - 3) // RING

            def step(r, n):
                turned_split_lo(r * RING + (n + 3), (n + 3) % RING)
                shift2(r * RING + n, n)
                add_gathered(r * RING + (n + 1), r + (n + 1) // RING, (n + 1) % RING)

            for n in range(RING):
                step(0, n)
            with dve.Fori(1, rounds) as r:
                for n in range(RING):
                    step(r, n)
            for k in range(rounds * RING, SORTED):
                if k + 3 < SORTED:
                    turned_split_lo(k + 3, (k + 3) % RING)
                shift2(k, k % RING)
                if k + 1 < SORTED:
                    add_gathered(k + 1, (k + 1) // RING, (k + 1) % RING)


def kernel(**inputs):
    import numpy as np
    import concourse.bacc as bacc
    from concourse.bass_utils import run_bass_kernel_spmd

    a = {name.replace("L0_", ""): np.asarray(value) for name, value in inputs.items()}
    by_partition = lambda name: a["attn_" + name].reshape(CH, P).T
    arrays = {
        "x": a["attn_x"],
        "xT": a["attn_x"].transpose(0, 2, 1),
        "w_square": np.stack([a["attn_Wk"].T, a["attn_Wv"].T, a["attn_Wr"].T, a["attn_Wo"].T]),
        "w_experts": a["ffn_W"].transpose(0, 2, 1),
        "vectors": np.stack([by_partition(n) for n in ("bk", "bv", "br", "tmk", "tmv", "tmr", "time_decay", "time_first")], axis=1),
        "bo": a["attn_bo"].reshape(1, H),
        "b_experts": a["ffn_b"],
        "wg": a["ffn_wg"],
    }
    arrays = {name: np.ascontiguousarray(value) for name, value in arrays.items()}
    nc = bacc.Bacc("TRN2", target_bir_lowering=False, num_devices=1)
    aps = [nc.dram_tensor(name, value.shape, mybir.dt.from_np(value.dtype), kind="ExternalInput").ap()
           for name, value in arrays.items()]
    out = nc.dram_tensor("out", (BATCH, TIME, H), F32, kind="ExternalOutput").ap()
    build(nc, *aps, out)
    result = run_bass_kernel_spmd(nc, [arrays], core_ids=[0])
    return result.results[0]["out"]
```

```python
from contextlib import ExitStack

import concourse.bass as bass
from concourse import mybir

ALU = mybir.AluOpType
ACT = mybir.ActivationFunctionType
AX_X = mybir.AxisListType.X
F32 = mybir.dt.float32
F32R = mybir.dt.float32r
I32 = mybir.dt.int32
U32 = mybir.dt.uint32

P = 128
BATCH, TIME, H = 4, 1024, 512
EXPERTS = 8
CH = H // P
TB = 512
HALVES = TIME // TB
BLOCKS = BATCH * HALVES
PAIRS = CH // 2
GROUPS = BLOCKS * PAIRS
BANKS = 4
FILLS = 3 * CH
TPB = TB // P
TOKENS = BATCH * TIME
TILES = TOKENS // P
SORTED = TILES + EXPERTS - 1
LISTS = SORTED + SORTED % 2
RING = 6
PART = 8
ID_RING = 2 * RING
AHEAD = 5
EPS = 1e-5
EXPONENT_CAP = 27.0
SIGMOID_CAP = 2.0 ** 80
LN_SHIFT = 60
LN2 = 0.6931471805599453
START = -1e30
K, V, R, O = range(4)
HI, LO = range(2)
EXPERT_ORDER = (0, 3, 1, 4, 2, 5, 6, 7)
SQ, SA, SB = range(3)
BIAS_ROWS = 2 * EXPERTS + 2
VEC_BK, VEC_BV, VEC_BR, VEC_MK, VEC_MV, VEC_MR, VEC_DECAY, VEC_FIRST = range(8)


def wait(eng, sem, value):
    if not isinstance(value, int) or value > 0:
        eng.wait_ge(sem, value)


class Block:

    def __init__(self, i, batch, half, first=False, last=False):
        self.i, self.batch, self.half, self.first, self.last = i, batch, half, first, last


def walk(eng, step, block_loop):
    step(Block(0, 0, 0, first=True))
    with block_loop(0, BATCH - 1) as b:
        step(Block(b * 2 + 1, b, 1))
        step(Block(b * 2 + 2, b + 1, 0))
    step(Block(BLOCKS - 1, BATCH - 1, 1, last=True))


def build(nc, x, xT, w_square, w_experts, vectors, bo, b_experts, wg, out):
    x1_rows = nc.dram_tensor("x1_rows", [TOKENS + 1, H], F32, kind="Internal").ap()

    with ExitStack() as ctx:
        cursor = [0]

        def place(name, shape, dtype, at=None):
            size = 4
            for n in shape[1:]:
                size *= n
            size = (size + 31) // 32 * 32
            offset = cursor[0] if at is None else at
            if at is None:
                cursor[0] += size
            return nc.alloc_sbuf_tensor_at(name, shape, dtype, offset=offset)

        base = nc.sbuf_base + (-nc.sbuf_base) % 32
        cursor[0] = base
        mat = 2 * CH * H * 4
        w_kvr = place("w_kvr", [P, 3, 2, CH, H], F32R)
        mixed = place("mixed", [P, 3, 2, CH, TB], F32R)
        w_o = place("w_o", [P, 2, CH, H], F32R)
        rw = place("rw", [P, 2, CH, TB], F32R)
        w_e_bytes = EXPERTS * mat
        unsplit = place("unsplit", [P, 3, 2, CH, TB], F32, at=base + 3 * mat)
        rw_unsplit = place("rw_unsplit", [P, 2, CH, TB], F32, at=base + 7 * mat)
        diff_at = cursor[0]
        diff = place("diff", [P, CH, TB], F32)
        xb_at = cursor[0]
        xb = place("xb", [P, CH, TB + 1], F32)
        temps_at = cursor[0]
        kd = place("kd", [P, 2, 2, TB], F32)
        vn = place("vn", [P, 2, 2, TB], F32)
        er = place("er", [P, 2, 2, TB], F32)
        state_at = cursor[0]
        state = place("state", [P, 3, 2, TB + 1], F32)
        e12 = place("e12", [P, 2, 2, TB], F32)
        rows_at = cursor[0]
        rows = place("rows", [P, TPB, H], F32)
        x1T = place("x1T", [P, CH, P], F32)
        bias_rows = place("bias_rows", [BIAS_ROWS, H], F32R)
        sel_bo = place("sel_bo", [BIAS_ROWS, P], F32R)
        ident = place("ident", [P, P], F32)
        vec = place("vec", [P, 8, CH], F32)
        wgs = place("wgs", [P, CH, EXPERTS], F32)
        wdec = place("wdec", [P, CH], F32)
        uw = place("uw", [P, CH], F32)
        nbr = place("nbr", [P, CH], F32)
        start_state = place("start_state", [P, 3, 2], F32)
        carry = place("carry", [P, 2, 3, 2], F32)
        bn = place("bn", [P, TPB, 6], F32)
        stats = place("stats", [P, TPB, 2], F32)
        rstd = place("rstd", [P, TPB], F32)
        nmr = place("nmr", [P, TPB], F32)
        eps_t = place("eps_t", [P, 1], F32)
        cap_t = place("cap_t", [P, 1], F32)
        part = place("part", [P, 1], F32)
        part8 = place("part8", [P, 1], F32)
        behind = place("behind", [P, P], F32R)
        ones = place("ones", [P, P], F32R)
        filled = place("filled", [P, P], F32)
        iota_q = place("iota_q", [P, P], F32)
        segment = place("segment", [P, EXPERTS, TILES], F32)
        steps = place("steps", [P, EXPERTS, TILES], F32)
        iota_k = place("iota_k", [P, LISTS], F32)
        token1 = place("token1", [P, TILES], F32)
        rank8 = place("rank8", [P, EXPERTS], F32)
        gate = place("gate", [P, TILES], F32)
        gate_parts = place("gate_parts", [P, 2, TILES], F32R)
        assert cursor[0] <= nc.sbuf_usable_end, cursor[0]
        w_raw = [place(f"w_raw{m}", [P, CH, H], F32, at=at)
                 for m, at in enumerate((temps_at, temps_at + 4 * 4 * TB, temps_at + 4 * 8 * TB, rows_at))]
        raw_at = state_at
        b_raw = place("b_raw", [EXPERTS, H], F32, at=raw_at)
        b_split = place("b_split", [EXPERTS, 2, H], F32R, at=raw_at + 4 * H)
        bo_raw = place("bo_raw", [1, H], F32, at=raw_at + 4 * 3 * H)
        bo_split = place("bo_split", [1, 2, H], F32R, at=raw_at + 4 * 4 * H)
        zero_row = place("zero_row", [1, H], F32, at=raw_at + 4 * 6 * H)
        assert raw_at + 4 * 7 * H <= rows_at
        w_e = place("w_e", [P, EXPERTS, 2, CH, H], F32R, at=base)
        assert w_e_bytes == diff_at - base
        we_raw = [place(f"we_raw{n}", [P, CH, H], F32, at=at) for n, at in enumerate((diff_at, xb_at))]
        xgT = place("xgT", [P, 3, 2, CH, P], F32R, at=diff_at)
        assert 4 * 3 * 2 * CH * P <= temps_at - diff_at
        x1T_last = place("x1T_last", [P, TPB, CH, P], F32, at=temps_at)
        cursor[0] = temps_at
        place_q = place("place_q", [P, TILES, P], F32R)
        place_k = place("place_k", [P, TILES, LISTS], F32)
        xg_at = cursor[0]
        place_list = place("place_list", [P, TILES, 3, LISTS], F32R)
        arrays_at = cursor[0]
        cursor[0] = temps_at
        yo = place("yo", [P, RING, H], F32)
        assert cursor[0] <= xg_at
        xg = place("xg", [P, RING, H], F32, at=xg_at)
        assert xg_at + 4 * RING * H <= rows_at
        cursor[0] = arrays_at
        lg = place("lg", [P, TILES, EXPERTS], F32)
        hot = place("hot", [P, EXPERTS, TILES], F32R)
        gate_e = place("gate_e", [P, TILES, EXPERTS], F32)
        work = place("work", [P, EXPERTS, TILES], F32)
        place_e = place("place_e", [P, EXPERTS, TILES], F32)
        mx = place("mx", [P, TILES], F32)
        chosen = place("chosen", [P, TILES], F32)
        sums = place("sums", [P, TILES], F32)
        dest = place("dest", [P, TILES], F32)
        dest_i = place("dest_i", [P, 3, TILES], I32)
        dest_f = place("dest_f", [P, 2, TILES], F32)
        ntiles = place("ntiles", [P, EXPERTS], F32)
        ends = place("ends", [P, EXPERTS], F32)
        starts = place("starts", [P, EXPERTS], F32)
        after = place("after", [P, SORTED, EXPERTS], F32)
        assert cursor[0] <= rows_at, (cursor[0], rows_at)
        cursor[0] = rows_at
        tile_e = place("tile_e", [P, SORTED], F32)
        tile_ei = place("tile_ei", [P, SORTED], I32)
        gates = place("gates", [P, SORTED], F32)
        empty = place("empty", [P, SORTED], F32)
        ids = place("ids", [P, SORTED], U32)
        id_now = place("id_now", [P, ID_RING, 1], U32)
        bn2 = place("bn2", [P, RING, 6], F32)
        stats2 = place("stats2", [P, RING, 2], F32)
        rstd2 = place("rstd2", [P, RING], F32)
        nmr2 = place("nmr2", [P, RING], F32)
        sel_e = place("sel_e", [BIAS_ROWS, 3, P], F32R)
        assert cursor[0] <= rows_at + 4 * (TPB * H + CH * P), cursor[0] - rows_at

        proj = ctx.enter_context(nc.psum_tensor("proj", [P, 4, TB], F32))
        y_ps = ctx.enter_context(nc.psum_tensor("y_ps", [P, 2, H], F32))
        t_ps = ctx.enter_context(nc.psum_tensor("t_ps", [P, CH, P], F32))
        lg_ps = ctx.enter_context(nc.psum_tensor("lg_ps", [P, TILES, EXPERTS], F32))

        y_banks = [y_ps[:, 0, :], y_ps[:, 1, :], proj[:, 0, :], proj[:, 1, :]]
        turn_banks = [proj[:, 2, :], proj[:, 3, :], t_ps[:].rearrange("p c q -> p (c q)"), proj[:, 0, :]]
        list_ps = lg_ps[:].rearrange("p t e -> p (t e)")[:, 0:3 * LISTS]
        turned_ps = [t_ps[:], proj[:, 0, :].rearrange("p (c q) -> p c q", c=CH)]

        def sem(name):
            return ctx.enter_context(nc.semaphore(name))

        waits_passed = sem("waits_passed")
        vec_loaded, w_loaded = sem("vec_loaded"), {n: sem(f"w_loaded{n}") for n in (V, R, O)}
        x_first, w_k_loaded = [sem(f"x_first{n}") for n in range(2)], [sem(f"w_k_loaded{n}") for n in range(2)]
        b_loaded, wg_loaded, bias_moved, zero_stored = sem("b_loaded"), sem("wg_loaded"), sem("bias_moved"), sem("zero_stored")
        consts_set, decay_exp, vec_ready = sem("consts_set"), sem("decay_exp"), sem("vec_ready")
        w_hi, w_lo, b_hi, b_lo = sem("w_hi"), sem("w_lo"), sem("b_hi"), sem("b_lo")
        ident_zero, ident_ready, sel_ready = sem("ident_zero"), sem("ident_ready"), sem("sel_ready")
        x_loaded, x_padded, diffed, mixed_f32 = sem("x_loaded"), sem("x_padded"), sem("diffed"), sem("mixed_f32")
        mixed_hi, mixed_lo = sem("mixed_hi"), sem("mixed_lo")
        proj_filled, proj_moved = sem("proj_filled"), sem("proj_moved")
        state_in, maxed, d_ready, capped = sem("state_in"), sem("maxed"), sem("d_ready"), sem("capped")
        clipped, e12_ready, big_e = sem("clipped"), sem("e12_ready"), sem("big_e")
        b_scanned, a_scanned, carried = sem("b_scanned"), sem("a_scanned"), sem("carried")
        ev_ready, big_ev, r_capped = sem("ev_ready"), sem("big_ev"), sem("r_capped")
        num_ready, den_part, den_ready = sem("num_ready"), sem("den_part"), sem("den_ready")
        den_ln, recip_guess, guess_tried, newton = sem("den_ln"), sem("recip_guess"), sem("guess_tried"), sem("newton")
        wkv_done, rw_hi, rw_lo = sem("wkv_done"), sem("rw_hi"), sem("rw_lo")
        row_loaded = [sem(f"row_loaded{j}") for j in range(TPB)]
        row_stored = [sem(f"row_stored{j}") for j in range(TPB)]
        y_filled, y_taken, bn_done, stats_done = sem("y_filled"), sem("y_taken"), sem("bn_done"), sem("stats_done")
        row_turned, x1T_moved = sem("row_turned"), sem("x1T_moved")
        var_ln, rstd_ready, nmr_ready, x1_ready = sem("var_ln"), sem("rstd_ready"), sem("nmr_ready"), sem("x1_ready")
        logits_done = sem("logits_done")
        route_const, routed, hot_ready, shifted = sem("route_const"), sem("routed"), sem("hot_ready"), sem("shifted")
        tile_placed, gate_split, gate_placed = sem("tile_placed"), sem("gate_split"), sem("gate_placed")
        gate_exp, counted, placed, listed = sem("gate_exp"), sem("counted"), sem("placed"), sem("listed")
        ids_ready, tiles_ready = sem("ids_ready"), sem("tiles_ready")
        we_loaded = [sem(f"we_loaded{n}") for n in range(2)]
        we_hi, we_lo = sem("we_hi"), [sem(f"we_lo{n}") for n in range(2)]
        id_set, gathered = sem("id_set"), [sem(f"gathered{n}") for n in range(RING)]
        turned, turned_hi, turned_lo, sel_set = sem("turned"), sem("turned_hi"), sem("turned_lo"), sem("sel_set")
        expert_filled, bn2_done, stats2_done = sem("expert_filled"), sem("bn2_done"), sem("stats2_done")
        var2_ln, rstd2_ready, nmr2_ready, out_ready = (
            sem("var2_ln"), sem("rstd2_ready"), sem("nmr2_ready"), sem("out_ready"))
        scattered = [sem(f"scattered{n}") for n in range(RING)]

        def wait_apart(eng, sem, value):
            if not isinstance(value, int) or value > 0:
                eng.wait_ge(sem, value)
                if not isinstance(value, int):
                    eng.sem_inc(waits_passed, 1)

        def try_guess(eng, i, p):
            g = i * 2 + p
            eng.wait_ge(recip_guess, g + 1)
            eng.tensor_tensor(kd[:, p], kd[:, p], er[:, p], ALU.mult).then_inc(guess_tried, 1)

        def rwkv_lo(eng, i, p):
            eng.wait_ge(rw_hi, i * 2 + (p + 1))
            eng.tensor_tensor(rw[:, LO, 2 * p:2 * p + 2, :], rw_unsplit[:, LO, 2 * p:2 * p + 2, :],
                              rw[:, HI, 2 * p:2 * p + 2, :].bitcast(F32), ALU.subtract).then_inc(rw_lo, 1)

        def expert_lo(eng, q):
            e = EXPERT_ORDER[q]
            eng.wait_ge(we_hi, q + 1)
            eng.tensor_tensor(w_e[:, e, LO], we_raw[q % 2][:], w_e[:, e, HI].bitcast(F32),
                              ALU.subtract).then_inc(we_lo[q % 2], 1)

        block = ctx.enter_context(nc.Block())

        xT_v = xT.rearrange("b (c p) t -> b p c t", p=P)
        x_v = x.rearrange("b (n p) h -> (b n) p h", p=P)
        x1_v = x1_rows[0:TOKENS, :].rearrange("(n p) h -> n p h", p=P)
        w_v = w_square.rearrange("m (c p) o -> m p c o", p=P)
        we_v = w_experts.rearrange("e (c p) o -> e p c o", p=P)
        out_v = out.rearrange("b t h -> (b t) h")

        @block.sync
        def _(sp):
            def load_x(n, batch, half):
                if half == 0:
                    sp.dma_start(xb[:, :, 1:], xT_v[batch, :, :, 0:TB]).then_inc(x_loaded, 16)
                else:
                    sp.dma_start(xb[:], xT_v[batch, :, :, TB - 1:]).then_inc(x_loaded, 16)

            def load_rows(n, first):
                for j in range(TPB):
                    if not first:
                        wait_apart(sp, row_turned, n * TPB + (j + 1 - TPB))
                        wait_apart(sp, row_stored[j], n * 16)
                    sp.dma_start(rows[:, j], x_v[n * TPB + j]).then_inc(row_loaded[j], 16)

            def store_rows(n):
                for j in range(TPB):
                    wait_apart(sp, x1_ready, n * TPB + (j + 1))
                    sp.dma_start(x1_v[n * TPB + j], rows[:, j]).then_inc(row_stored[j], 16)

            def load_expert(q):
                wait(sp, we_lo[q % 2], q // 2)
                sp.dma_start(we_raw[q % 2][:], we_v[EXPERT_ORDER[q]]).then_inc(we_loaded[q % 2], 16)

            def step(s):
                if s.first:
                    sp.wait_ge(w_lo, 5)
                    load_rows(0, first=True)
                    return
                if not s.last:
                    wait_apart(sp, mixed_f32, s.i * 6 + 6)
                    load_x(s.i + 1, s.batch + s.half, 1 - s.half)
                else:
                    sp.wait_ge(mixed_f32, BLOCKS * 6)
                    load_expert(0)
                    load_expert(1)
                store_rows(s.i - 1)
                load_rows(s.i, first=False)

            sp.dma_start(vec[:], vectors).then_inc(vec_loaded, 16)
            for hp in range(2):
                half = slice(2 * hp, 2 * hp + 2)
                sp.dma_start(xb[:, half, 1:], xT_v[0, :, half, 0:TB]).then_inc(x_first[hp], 16)
            for hp in range(2):
                half = slice(2 * hp, 2 * hp + 2)
                sp.dma_start(w_raw[K][:, half], w_v[K][:, half]).then_inc(w_k_loaded[hp], 16)
            sp.dma_start(b_raw[:], b_experts).then_inc(b_loaded, 16)
            sp.dma_start(bo_raw[:], bo).then_inc(b_loaded, 16)
            for n in (V, R, O):
                sp.dma_start(w_raw[n][:], w_v[n]).then_inc(w_loaded[n], 16)
            sp.dma_start(wgs[:], wg.rearrange("(c p) e -> p c e", p=P)).then_inc(wg_loaded, 16)
            sp.wait_ge(consts_set, 1)
            sp.dma_start(x1_rows[TOKENS:TOKENS + 1, :], zero_row[:]).then_inc(zero_stored, 16)
            sp.wait_ge(b_lo, 2)
            for s in range(2):
                sp.dma_start(bias_rows[s * EXPERTS:(s + 1) * EXPERTS, :].bitcast(F32), b_split[:, s, :].bitcast(F32)).then_inc(bias_moved, 16)
                sp.dma_start(bias_rows[2 * EXPERTS + s:2 * EXPERTS + s + 1, :].bitcast(F32), bo_split[:, s, :].bitcast(F32)).then_inc(bias_moved, 16)
            sp.wait_ge(mixed_f32, 6)
            load_x(1, 0, 1)
            walk(sp, step, sp.Fori)
            for q in range(2, 6):
                load_expert(q)
            store_rows(BLOCKS - 1)
            for q in range(6, EXPERTS):
                load_expert(q)

        @block.tensor
        def _(pe):
            def project(s, m, p, c):
                n = 4 * m + 2 * p + c
                if p == 0 and c == 0:
                    if not (s.first and m == K):
                        pe.wait_ge(mixed_lo, s.i * 6 + (2 * m + 2))
                    if s.first and m != K:
                        pe.wait_ge(w_lo, m + 2)
                wait(pe, proj_moved, s.i * FILLS + (n + 1 - BANKS))
                o = (2 * p + c) * P
                k = 0
                for h in range(CH):
                    if s.first and n == 0 and h % 2 == 0:
                        pe.wait_ge(w_lo, h // 2 + 1)
                        pe.wait_ge(mixed_lo, h // 2 + 1)
                    for a, bb in ((HI, HI), (HI, LO), (LO, HI)):
                        mm = pe.matmul(proj[:, n % BANKS, :], w_kvr[:, m, a, h, o:o + P], mixed[:, m, bb, h, :],
                                       start=(k == 0), stop=(k == 3 * CH - 1))
                        k += 1
                mm.then_inc(proj_filled, 1)

            def project_out(n, j):
                pe.wait_ge(rw_lo, n * 2 + 2)
                if isinstance(n, int) and n == 0 and j == 0:
                    pe.wait_ge(bias_moved, 64)
                pe.wait_ge(y_taken, n * TPB + (j + 1))
                pe.matmul(y_ps[:, j % 2, :], sel_bo[:], bias_rows[:], start=True, stop=False)
                for c in range(CH):
                    for a, bb in ((HI, HI), (HI, LO), (LO, HI)):
                        mm = pe.matmul(y_ps[:, j % 2, :], rw[:, a, c, j * P:(j + 1) * P], w_o[:, bb, c, :],
                                       start=False, stop=(c == CH - 1 and (a, bb) == (LO, HI)))
                mm.then_inc(y_filled, 1)

            def turn_rows(n, j):
                pe.wait_ge(x1_ready, n * TPB + (j + 1))
                for c in range(CH):
                    mm = pe.transpose(t_ps[:, c, :], rows[:, j, c * P:(c + 1) * P], ident[:])
                mm.then_inc(row_turned, 1)

            def logits(n, j, tile):
                if isinstance(n, int) and n == 0 and j == 0:
                    pe.wait_ge(wg_loaded, 16)
                pe.wait_ge(x1T_moved, n * TPB + (j + 1))
                for c in range(CH):
                    mm = pe.matmul(lg_ps[:, tile, :], x1T[:, c, :], wgs[:, c, :], start=(c == 0), stop=(c == CH - 1))
                mm.then_inc(logits_done, 1)

            def step(s):
                project(s, K, 0, 0)
                project(s, K, 0, 1)
                project(s, K, 1, 0)
                project(s, K, 1, 1)
                project(s, V, 0, 0)
                project(s, V, 0, 1)
                if not s.first:
                    project_out(s.i - 1, 0)
                    project_out(s.i - 1, 1)
                    project_out(s.i - 1, 2)
                    project_out(s.i - 1, 3)
                project(s, V, 1, 0)
                project(s, V, 1, 1)
                if not s.first:
                    turn_rows(s.i - 1, 0)
                project(s, R, 0, 0)
                if not s.first:
                    logits(s.i - 1, 0, (s.i - 1) * TPB + 0)
                    turn_rows(s.i - 1, 1)
                project(s, R, 0, 1)
                if not s.first:
                    logits(s.i - 1, 1, (s.i - 1) * TPB + 1)
                if not s.first and not s.last:
                    turn_rows(s.i - 1, 2)
                project(s, R, 1, 0)
                if not s.first and not s.last:
                    logits(s.i - 1, 2, (s.i - 1) * TPB + 2)
                    turn_rows(s.i - 1, 3)
                project(s, R, 1, 1)
                if not s.first and not s.last:
                    logits(s.i - 1, 3, (s.i - 1) * TPB + 3)
                if s.last:
                    turn_rows(s.i - 1, 2)
                    logits(s.i - 1, 2, (s.i - 1) * TPB + 2)
                    turn_rows(s.i - 1, 3)
                    logits(s.i - 1, 3, (s.i - 1) * TPB + 3)

            pe.wait_ge(sel_ready, 1)
            pe.wait_ge(ident_ready, 1)
            walk(pe, step, pe.Fori)
            last = BLOCKS - 1
            for pair in range(PAIRS):
                pe.wait_ge(rw_lo, last * 2 + (pair + 1))
                if pair == 0:
                    pe.wait_ge(y_taken, last * TPB + 2)
                    pe.wait_ge(proj_moved, BLOCKS * FILLS)
                for j in range(TPB):
                    if pair == 0:
                        pe.matmul(y_banks[j], sel_bo[:], bias_rows[:], start=True, stop=False)
                    for c in range(2 * pair, 2 * pair + 2):
                        for a, bb in ((HI, HI), (HI, LO), (LO, HI)):
                            mm = pe.matmul(y_banks[j], rw[:, a, c, j * P:(j + 1) * P], w_o[:, bb, c, :],
                                           start=False, stop=(c == CH - 1 and (a, bb) == (LO, HI)))
                    if pair == 1:
                        mm.then_inc(y_filled, 1)

            def turn_last(j):
                pe.wait_ge(x1_ready, last * TPB + (j + 1))
                for c in range(CH):
                    mm = pe.transpose(turn_banks[j][:, c * P:(c + 1) * P], rows[:, j, c * P:(c + 1) * P], ident[:])
                mm.then_inc(row_turned, 1)

            turn_last(0)
            for j in range(TPB):
                if j + 1 < TPB:
                    turn_last(j + 1)
                pe.wait_ge(x1T_moved, last * TPB + (j + 1))
                for c in range(CH):
                    mm = pe.matmul(lg_ps[:, last * TPB + j, :], x1T_last[:, j, c, :], wgs[:, c, :], start=(c == 0), stop=(c == CH - 1))
                mm.then_inc(logits_done, 1)

            n_te = EXPERTS * TILES
            pe.wait_ge(route_const, 1)
            pe.wait_ge(hot_ready, 1)
            hot_all = hot[:].rearrange("p e t -> p (e t)")
            pe.matmul(y_ps[:, 0, 0:n_te], behind[:], hot_all, start=True, stop=True)
            pe.matmul(y_ps[:, 1, 0:n_te], ones[:], hot_all, start=True, stop=True).then_inc(counted, 1)
            for t in range(TILES):
                if t % PART == 0:
                    pe.wait_ge(placed, t // PART + 1)
                    pe.wait_ge(gate_placed, t // PART + 1)
                mm = pe.matmul(list_ps, place_q[:, t, :], place_list[:, t].rearrange("p w k -> p (w k)"),
                               start=(t == 0), stop=(t == TILES - 1))
            mm.then_inc(listed, 1)

            def turn(k, r, n):
                pe.wait_ge(gathered[n], r * 16 + 16)
                wait(pe, turned_lo, k - 1)
                for c in range(CH):
                    mm = pe.transpose(turned_ps[n % 2][:, c, :], xg[:, n, c * P:(c + 1) * P], ident[:])
                mm.then_inc(turned, 1)

            def expert(k, n):
                parity, third = n % 2, n % 3
                e = pe.value_load(tile_ei[0:1, bass.ds(k, 1)], min_val=0, max_val=EXPERTS - 1)
                pe.wait_ge(turned_lo, k + 1)
                pe.wait_ge(sel_set, k + 1)
                pe.wait_ge(y_taken, k + (TILES + 1))
                pe.matmul(y_ps[:, parity, :], sel_e[:, third, :], bias_rows[:], start=True, stop=False)
                for c in range(CH):
                    for a, bb in ((HI, HI), (HI, LO), (LO, HI)):
                        mm = pe.matmul(y_ps[:, parity, :], xgT[:, third, a, c, :],
                                       w_e[:, bass.ds(e, 1), bb, c, :].rearrange("p u o -> p (u o)"),
                                       start=False, stop=(c == CH - 1 and (a, bb) == (LO, HI)))
                mm.then_inc(expert_filled, 1)

            pe.wait_ge(tiles_ready, 1)
            pe.wait_ge(ids_ready, 1)
            for n in range(2):
                pe.wait_ge(we_lo[n], EXPERTS // 2)
            turn(0, 0, 0)
            turn(1, 0, 1)

            with pe.Fori(0, SORTED // RING) as r:
                for n in range(RING):
                    turn(r * RING + (n + 2), r + (n + 2) // RING, (n + 2) % RING)
                    expert(r * RING + n, n)
            for k in range(SORTED // RING * RING, SORTED):
                if k + 2 < SORTED:
                    turn(k + 2, (k + 2) // RING, (k + 2) % RING)
                expert(k, k % RING)

        @block.scalar
        def _(act):
            def mix_hi(n, m, hp):
                act.wait_ge(mixed_f32, n * 6 + (2 * m + hp + 1))
                act.activation(mixed[:, m, HI, 2 * hp:2 * hp + 2, :], unsplit[:, m, LO, 2 * hp:2 * hp + 2, :],
                               ACT.Copy).then_inc(mixed_hi, 1)

            def evacuate(s, m, p, c):
                n = 4 * m + 2 * p + c
                bank = proj[:, n % BANKS, :]
                if s.first and n % CH == 0:
                    act.wait_ge(w_lo, m + 2)
                act.wait_ge(proj_filled, s.i * FILLS + (n + 1))
                if not s.first:
                    act.wait_ge(wkv_done, s.i * 2 + (p - 1))
                col = slice(2 * p + c, 2 * p + c + 1)
                if m == K:
                    ins = act.activation(kd[:, p, c, :], bank, ACT.Identity, bias=vec[:, VEC_BK, col])
                elif m == V:
                    ins = act.activation(vn[:, p, c, :], bank, ACT.Identity, bias=vec[:, VEC_BV, col])
                else:
                    ins = act.activation(er[:, p, c, :], bank, ACT.Exp, bias=nbr[:, col], scale=-1.0)
                ins.then_inc(proj_moved, 1)

            def decays(s, p):
                g = s.i * 2 + p
                act.wait_ge(clipped, g * 2 + 1)
                act.activation(e12[:, 0], e12[:, 0], ACT.Exp).then_inc(e12_ready, 1)
                act.wait_ge(clipped, g * 2 + 2)
                act.activation(e12[:, 1], e12[:, 1], ACT.Exp, scale=-1.0).then_inc(e12_ready, 1)

            def weight_now(s, p):
                g = s.i * 2 + p
                act.wait_ge(capped, g * 2 + 2)
                act.activation(kd[:, p], kd[:, p], ACT.Exp, scale=-1.0).then_inc(big_e, 1)

            def rwkv_hi(i, p):
                act.wait_ge(wkv_done, i * 2 + (p + 1))
                act.activation(rw[:, HI, 2 * p:2 * p + 2, :], rw_unsplit[:, LO, 2 * p:2 * p + 2, :], ACT.Copy).then_inc(rw_hi, 1)

            def reciprocal_guess(i, p):
                g = i * 2 + p
                act.wait_ge(den_ready, g + 1)
                act.activation(er[:, p], kd[:, p], ACT.Ln, scale=2.0 ** -LN_SHIFT).then_inc(den_ln, 1)
                act.wait_ge(den_ln, g + 1)
                act.activation(er[:, p], er[:, p], ACT.Exp, bias=cap_t[:], scale=-1.0).then_inc(recip_guess, 1)

            def norm(n):
                act.wait_ge(stats_done, n * TPB + TPB)
                act.activation(rstd[:], stats[:, :, 1], ACT.Ln, bias=eps_t[:]).then_inc(var_ln, 1)
                act.wait_ge(var_ln, n + 1)
                act.activation(rstd[:], rstd[:], ACT.Exp, scale=-0.5).then_inc(rstd_ready, 1)
                act.wait_ge(nmr_ready, n + 1)
                for j in range(TPB):
                    act.activation(rows[:, j], rows[:, j], ACT.Identity, bias=nmr[:, j:j + 1],
                                   scale=rstd[:, j:j + 1]).then_inc(x1_ready, 1)

            def move_turned(n, j):
                act.wait_ge(row_turned, n * TPB + (j + 1))
                act.activation(x1T[:], t_ps[:], ACT.Copy).then_inc(x1T_moved, 1)

            def expert_hi(q):
                e = EXPERT_ORDER[q]
                act.wait_ge(we_loaded[q % 2], q // 2 * 16 + 16)
                act.activation(w_e[:, e, HI], we_raw[q % 2][:], ACT.Copy).then_inc(we_hi, 1)

            def step(s):
                if not s.first:
                    reciprocal_guess(s.i - 1, 1)
                    mix_hi(s.i, R, 0)
                evacuate(s, K, 0, 0)
                evacuate(s, K, 0, 1)
                if not s.first:
                    mix_hi(s.i, R, 1)
                    rwkv_hi(s.i - 1, 1)
                evacuate(s, K, 1, 0)
                decays(s, 0)
                evacuate(s, K, 1, 1)
                weight_now(s, 0)
                evacuate(s, V, 0, 0)
                evacuate(s, V, 0, 1)
                if not s.last:
                    mix_hi(s.i + 1, K, 0)
                    mix_hi(s.i + 1, K, 1)
                if not s.first:
                    norm(s.i - 1)
                    move_turned(s.i - 1, 0)
                evacuate(s, V, 1, 0)
                if not s.first:
                    move_turned(s.i - 1, 1)
                decays(s, 1)
                evacuate(s, V, 1, 1)
                evacuate(s, R, 0, 0)
                evacuate(s, R, 0, 1)
                if not s.first and not s.last:
                    move_turned(s.i - 1, 2)
                weight_now(s, 1)
                if not s.last:
                    mix_hi(s.i + 1, V, 0)
                reciprocal_guess(s.i, 0)
                if not s.last:
                    mix_hi(s.i + 1, V, 1)
                if not s.first and not s.last:
                    move_turned(s.i - 1, 3)
                evacuate(s, R, 1, 0)
                evacuate(s, R, 1, 1)
                if s.last:
                    move_turned(s.i - 1, 2)
                    expert_hi(0)
                    move_turned(s.i - 1, 3)
                    expert_hi(1)
                if not s.last:
                    rwkv_hi(s.i, 0)
                if s.last:
                    reciprocal_guess(s.i, 1)

            act.preload_act_table_set("natural_log_exp_and_others")
            act.wait_ge(vec_loaded, 16)
            act.activation(wdec[:], vec[:, VEC_DECAY, :], ACT.Exp).then_inc(decay_exp, 1)
            for hp in range(2):
                act.wait_ge(w_k_loaded[hp], 16)
                act.activation(w_kvr[:, K, HI, 2 * hp:2 * hp + 2], w_raw[K][:, 2 * hp:2 * hp + 2], ACT.Copy).then_inc(w_hi, 1)
            mix_hi(0, K, 0)
            mix_hi(0, K, 1)
            act.wait_ge(b_loaded, 32)
            act.activation(b_split[:, HI], b_raw[:], ACT.Copy).then_inc(b_hi, 1)
            act.activation(bo_split[:, HI], bo_raw[:], ACT.Copy).then_inc(b_hi, 1)
            for m in (V, R, O):
                act.wait_ge(w_loaded[m], 16)
                dst = w_o[:, HI] if m == O else w_kvr[:, m, HI]
                act.activation(dst, w_raw[m][:], ACT.Copy).then_inc(w_hi, 1)
                if m != O:
                    mix_hi(0, m, 0)
                    mix_hi(0, m, 1)
            act.wait_ge(consts_set, 1)
            walk(act, step, act.Fori)
            last = BLOCKS - 1
            rwkv_hi(last, 0)
            rwkv_hi(last, 1)
            for q in range(2, 5):
                expert_hi(q)

            def norm_last(j):
                act.wait_ge(stats_done, last * TPB + (j + 1))
                act.activation(rstd[:, j:j + 1], stats[:, j, 1:2], ACT.Ln, bias=eps_t[:]).then_inc(var_ln, 1)
                act.wait_ge(var_ln, last + (j + 1))
                act.activation(rstd[:, j:j + 1], rstd[:, j:j + 1], ACT.Exp, scale=-0.5).then_inc(rstd_ready, 1)
                act.wait_ge(nmr_ready, last + (j + 1))
                act.activation(rows[:, j], rows[:, j], ACT.Identity, bias=nmr[:, j:j + 1],
                               scale=rstd[:, j:j + 1]).then_inc(x1_ready, 1)

            def move_last(j):
                act.wait_ge(row_turned, last * TPB + (j + 1))
                act.activation(x1T_last[:, j], turn_banks[j].rearrange("p (c q) -> p c q", c=CH), ACT.Copy).then_inc(x1T_moved, 1)

            norm_last(0)
            for j in range(1, TPB):
                norm_last(j)
                move_last(j - 1)
            move_last(TPB - 1)
            expert_hi(5)
            act.wait_ge(y_filled, TILES)
            expert_hi(6)
            act.wait_ge(shifted, 1)
            act.activation(gate_e[:], lg[:], ACT.Exp).then_inc(gate_exp, 1)
            expert_hi(7)

            def turned_split_hi(k, n):
                act.wait_ge(turned, k + 1)
                wait(act, expert_filled, k - 2)
                act.activation(xgT[:, n % 3, HI], turned_ps[n % 2], ACT.Copy).then_inc(turned_hi, 1)

            def norm2(k, n):
                act.wait_ge(stats2_done, k + 1)
                act.activation(rstd2[:, n:n + 1], stats2[:, n, 1:2], ACT.Ln, bias=eps_t[:]).then_inc(var2_ln, 1)
                act.wait_ge(var2_ln, k + 1)
                act.activation(rstd2[:, n:n + 1], rstd2[:, n:n + 1], ACT.Exp, scale=-0.5).then_inc(rstd2_ready, 1)
                act.wait_ge(nmr2_ready, k + 1)
                act.activation(yo[:, n], yo[:, n], ACT.Identity, bias=nmr2[:, n:n + 1],
                               scale=rstd2[:, n:n + 1]).then_inc(out_ready, 1)

            for n in range(2):
                act.wait_ge(we_lo[n], EXPERTS // 2)
            for k in range(3):
                turned_split_hi(k, k)
            rounds = (SORTED - 3) // RING
            with act.Fori(0, rounds) as r:
                for n in range(RING):
                    turned_split_hi(r * RING + (n + 3), (n + 3) % RING)
                    norm2(r * RING + n, n)
            for k in range(rounds * RING, SORTED):
                if k + 3 < SORTED:
                    turned_split_hi(k + 3, (k + 3) % RING)
                norm2(k, k % RING)

        @block.gpsimd
        def _(pool):
            def mix_lo(n, m, hp):
                pool.wait_ge(mixed_hi, n * 6 + (2 * m + hp + 1))
                pool.tensor_tensor(mixed[:, m, LO, 2 * hp:2 * hp + 2, :], unsplit[:, m, LO, 2 * hp:2 * hp + 2, :],
                                   mixed[:, m, HI, 2 * hp:2 * hp + 2, :].bitcast(F32),
                                   ALU.subtract).then_inc(mixed_lo, 1)

            def weigh_entry(s, p):
                g = s.i * 2 + p
                pool.wait_ge(b_scanned, g * 2 + 2)
                pool.wait_ge(proj_moved, s.i * FILLS + (4 * V + 2 * p + 2))
                pool.tensor_tensor(e12[:, 1], e12[:, 1], vn[:, p], ALU.mult).then_inc(ev_ready, 1)

            def weigh_now(s, p):
                g = s.i * 2 + p
                pool.wait_ge(big_e, g + 1)
                pool.wait_ge(ev_ready, g + 1)
                pool.tensor_tensor(vn[:, p], vn[:, p], kd[:, p], ALU.mult).then_inc(big_ev, 1)

            def step(s):
                if not s.first:
                    try_guess(pool, s.i - 1, 1)
                    mix_lo(s.i, R, 0)
                    rwkv_lo(pool, s.i - 1, 1)
                    mix_lo(s.i, R, 1)
                weigh_entry(s, 0)
                weigh_now(s, 0)
                if not s.last:
                    mix_lo(s.i + 1, K, 0)
                    mix_lo(s.i + 1, K, 1)
                weigh_entry(s, 1)
                weigh_now(s, 1)
                if s.last:
                    expert_lo(pool, 0)
                if not s.last:
                    try_guess(pool, s.i, 0)
                    mix_lo(s.i + 1, V, 0)
                    mix_lo(s.i + 1, V, 1)
                    rwkv_lo(pool, s.i, 0)
                if s.last:
                    expert_lo(pool, 1)

            pool.memset(ident[:], 0.0).then_inc(ident_zero, 1)
            pool.wait_ge(ident_zero, 1)
            pool.affine_select(out=ident[:], in_=ident[:], compare_op=ALU.not_equal, fill=1.0, base=0,
                               pattern=[[-1, P]], channel_multiplier=1).then_inc(ident_ready, 1)
            pool.iota(part[:], pattern=[[0, 1]], base=0, channel_multiplier=1,
                      allow_small_or_imprecise_dtypes=True).then_inc(ident_zero, 1)
            rc = []
            rc.append(pool.memset(filled[:], 0.0))
            rc.append(pool.memset(segment[:], 1.0))
            rc.append(pool.iota(iota_q[:], pattern=[[1, P]], base=0, channel_multiplier=0, allow_small_or_imprecise_dtypes=True))
            rc.append(pool.iota(steps[:], pattern=[[0, EXPERTS], [P, TILES]], base=0, channel_multiplier=0, allow_small_or_imprecise_dtypes=True))
            rc.append(pool.iota(iota_k[:], pattern=[[1, LISTS]], base=0, channel_multiplier=0, allow_small_or_imprecise_dtypes=True))
            rc.append(pool.iota(token1[:], pattern=[[P, TILES]], base=1, channel_multiplier=1, allow_small_or_imprecise_dtypes=True))
            rc.append(pool.iota(rank8[:], pattern=[[-1, EXPERTS]], base=EXPERTS, channel_multiplier=0, allow_small_or_imprecise_dtypes=True))
            rc[-1].then_inc(ident_zero, 1)
            pool.wait_ge(ident_zero, 3)
            pool.memset(segment[:, :, 0:1], 0.0)
            pool.affine_select(out=behind[:], in_=filled[:], compare_op=ALU.is_gt, fill=-1.0, base=0,
                               pattern=[[1, P]], channel_multiplier=-1).then_inc(ident_zero, 1)
            pool.wait_ge(ident_zero, 4)
            pool.memset(filled[:], 1.0).then_inc(ident_zero, 1)
            pool.wait_ge(ident_zero, 5)
            pool.tensor_copy(ones[:], filled[:]).then_inc(route_const, 1)
            for hp in range(2):
                pool.wait_ge(w_hi, hp + 1)
                half = slice(2 * hp, 2 * hp + 2)
                pool.tensor_tensor(w_kvr[:, K, LO, half], w_raw[K][:, half], w_kvr[:, K, HI, half].bitcast(F32), ALU.subtract).then_inc(w_lo, 1)
            for m in (V, R, O):
                pool.wait_ge(w_hi, m + 2)
                hi, lo = (w_o[:, HI], w_o[:, LO]) if m == O else (w_kvr[:, m, HI], w_kvr[:, m, LO])
                pool.tensor_tensor(lo, w_raw[m][:], hi.bitcast(F32), ALU.subtract).then_inc(w_lo, 1)
                if m in (V, R):
                    mix_lo(0, m, 0)
                    mix_lo(0, m, 1)
            walk(pool, step, pool.Fori)
            for q in range(3, 7):
                expert_lo(pool, q)

            pool.wait_ge(gate_split, 1)
            pool.wait_ge(tile_placed, 1)
            for t in range(0, TILES, PART):
                part_shape = [P, PART, 2, LISTS]
                pool.tensor_tensor(place_list[:, t:t + PART, 1:3, :], place_k[:, t:t + PART, None, :].to_broadcast(part_shape),
                                   gate_parts[:, :, t:t + PART].rearrange("p w t -> p t w").bitcast(F32)[:, :, :, None].to_broadcast(part_shape),
                                   ALU.mult).then_inc(gate_placed, 1)
            expert_lo(pool, 7)

            def gather(k, m):
                pool.tensor_copy(id_now[:, m, :], ids[:, bass.ds(k, 1)]).then_inc(id_set, 1)
                wait_apart(pool, id_set, k + 1)
                pool.indirect_dma_start(
                    out=xg[:, m % RING, :], out_offset=None, in_=x1_rows[:, :],
                    in_offset=bass.IndirectOffsetOnAxis(ap=id_now[:, m, :], axis=0)).then_inc(gathered[m % RING], 16)

            def scatter(k, m):
                wait_apart(pool, out_ready, k + 1)
                pool.indirect_dma_start(
                    out=out_v, out_offset=bass.IndirectOffsetOnAxis(ap=id_now[:, m, :], axis=0),
                    in_=yo[:, m % RING, :], in_offset=None, bounds_check=TOKENS - 1, oob_is_err=False).then_inc(scattered[m % RING], 16)

            pool.wait_ge(ids_ready, 1)
            pool.wait_ge(zero_stored, 16)
            for j in range(TPB):
                pool.wait_ge(row_stored[j], BLOCKS * 16)
            for k in range(AHEAD):
                gather(k, k)
            rounds = (SORTED - AHEAD) // ID_RING
            with pool.Fori(0, rounds) as r:
                for m in range(ID_RING):
                    pool.wait_ge(y_taken, r * ID_RING + (TILES + m + AHEAD - RING + 3))
                    gather(r * ID_RING + (m + AHEAD), (m + AHEAD) % ID_RING)
                    scatter(r * ID_RING + m, m)
            for k in range(rounds * ID_RING, SORTED):
                if k + AHEAD < SORTED:
                    pool.wait_ge(y_taken, TILES + k + AHEAD - RING + 3)
                    gather(k + AHEAD, (k + AHEAD) % ID_RING)
                scatter(k, k % ID_RING)
            for n in range(RING):
                pool.wait_ge(scattered[n], (SORTED - n + RING - 1) // RING * 16)

        @block.vector
        def _(dve):
            def difference(n, batch=None):
                wait(dve, mixed_f32, n * 6)
                if batch is not None:
                    dve.memset(xb[:, :, 0:1], 0.0).then_inc(x_padded, 1)
                    dve.wait_ge(x_padded, batch + 1)
                dve.wait_ge(x_loaded, n * 16)
                dve.tensor_tensor(diff[:], xb[:, :, 1:], xb[:, :, 0:TB], ALU.subtract).then_inc(diffed, 1)

            def mix_matrix(n, m, hp):
                if not (isinstance(n, int) and n == 0 and m == K):
                    dve.wait_ge(diffed, n + 2)
                wait(dve, proj_filled, n * FILLS + (4 * m + 4 - FILLS))
                for h in range(2 * hp, 2 * hp + 2):
                    ins = dve.scalar_tensor_tensor(out=unsplit[:, m, LO, h, :], in0=diff[:, h, :],
                                                   scalar=vec[:, VEC_MK + m, h:h + 1], in1=xb[:, h, 0:TB],
                                                   op0=ALU.mult, op1=ALU.add)
                ins.then_inc(mixed_f32, 1)

            def running_max(s, p):
                g = s.i * 2 + p
                wait(dve, num_ready, g)
                src = start_state[:] if s.half == 0 else carry[:, p]
                if s.half == 1:
                    dve.wait_ge(carried, s.i - 1 + (p + 1))
                dve.tensor_copy(state[:, :, :, 0], src).then_inc(state_in, 1)
                dve.wait_ge(state_in, g + 1)
                for c in range(2):
                    dve.wait_ge(proj_moved, s.i * FILLS + (4 * K + 2 * p + c + 1))
                    h = 2 * p + c
                    dve.tensor_tensor_scan(state[:, SQ, c, 1:], kd[:, p, c, :], wdec[:, h:h + 1].to_broadcast([P, TB]),
                                           state[:, SQ, c, 0:1], ALU.max, ALU.add).then_inc(maxed, 1)
                dve.wait_ge(maxed, g * 2 + 2)
                dve.tensor_tensor(kd[:, p], state[:, SQ, :, 0:TB], kd[:, p], ALU.subtract).then_inc(d_ready, 1)

            def clip(s, p):
                g = s.i * 2 + p
                dve.wait_ge(d_ready, g + 1)
                wait(dve, a_scanned, g * 2)
                dve.tensor_scalar(e12[:, 0], kd[:, p], 0.0, None, ALU.min).then_inc(clipped, 1)
                dve.tensor_scalar(e12[:, 1], kd[:, p], 0.0, None, ALU.max).then_inc(clipped, 1)
                dve.wait_ge(clipped, g * 2 + 2)
                for c in range(2):
                    h = 2 * p + c
                    dve.tensor_scalar(kd[:, p, c, :], kd[:, p, c, :], uw[:, h:h + 1], -EXPONENT_CAP,
                                      ALU.subtract, ALU.max).then_inc(capped, 1)

            def scan_den(s, p):
                g = s.i * 2 + p
                dve.wait_ge(e12_ready, g * 2 + 2)
                for c in range(2):
                    dve.tensor_tensor_scan(state[:, SB, c, 1:], e12[:, 0, c, :], e12[:, 1, c, :],
                                           state[:, SB, c, 0:1], ALU.mult, ALU.add).then_inc(b_scanned, 1)

            def scan_num(s, p):
                g = s.i * 2 + p
                dve.wait_ge(ev_ready, g + 1)
                for c in range(2):
                    dve.tensor_tensor_scan(state[:, SA, c, 1:], e12[:, 0, c, :], e12[:, 1, c, :],
                                           state[:, SA, c, 0:1], ALU.mult, ALU.add).then_inc(a_scanned, 1)

            def leave(s, p):
                g = s.i * 2 + p
                dve.wait_ge(big_ev, g + 1)
                dve.tensor_tensor(kd[:, p], kd[:, p], state[:, SB, :, 0:TB], ALU.add).then_inc(den_part, 1)
                dve.wait_ge(a_scanned, g * 2 + 2)
                dve.tensor_tensor(vn[:, p], vn[:, p], state[:, SA, :, 0:TB], ALU.add).then_inc(num_ready, 1)
                if s.half == 0:
                    dve.tensor_copy(carry[:, p], state[:, :, :, TB]).then_inc(carried, 1)

            def denominator(i, p):
                g = i * 2 + p
                dve.wait_ge(proj_moved, i * FILLS + (4 * R + 2 * p + 2))
                dve.tensor_scalar(er[:, p], er[:, p], SIGMOID_CAP, None, ALU.min).then_inc(r_capped, 1)
                dve.wait_ge(r_capped, g + 1)
                dve.wait_ge(den_part, g + 1)
                dve.scalar_tensor_tensor(out=kd[:, p], in0=er[:, p], scalar=1.0, in1=kd[:, p],
                                         op0=ALU.add, op1=ALU.mult).then_inc(den_ready, 1)

            def result(i, p):
                g = i * 2 + p
                dve.wait_ge(guess_tried, g + 1)
                dve.scalar_tensor_tensor(out=er[:, p], in0=kd[:, p], scalar=2.0, in1=er[:, p],
                                         op0=ALU.subtract, op1=ALU.mult).then_inc(newton, 1)
                dve.wait_ge(newton, g + 1)
                wait(dve, y_filled, i * TPB)
                dve.wait_ge(num_ready, g + 1)
                dve.scalar_tensor_tensor(out=rw_unsplit[:, LO, 2 * p:2 * p + 2, :], in0=vn[:, p], scalar=-1.0,
                                         in1=er[:, p], op0=ALU.mult, op1=ALU.mult).then_inc(wkv_done, 1)

            def add_rows(n, j, bank=None):
                dve.wait_ge(row_loaded[j], n * 16 + 16)
                dve.wait_ge(y_filled, n * TPB + (j + 1))
                dve.tensor_tensor(rows[:, j], rows[:, j], y_ps[:, j % 2, :] if bank is None else bank, ALU.add).then_inc(y_taken, 1)

            def shift(n):
                dve.wait_ge(rstd_ready, n + 1)
                dve.scalar_tensor_tensor(out=nmr[:], in0=stats[:, :, 0], scalar=-1.0, in1=rstd[:],
                                         op0=ALU.mult, op1=ALU.mult).then_inc(nmr_ready, 1)

            def statistics(n, j):
                dve.wait_ge(y_taken, n * TPB + (j + 3))
                dve.bn_stats(bn[:, j, :], rows[:, j]).then_inc(bn_done, 1)

            def aggregate(n, j):
                wait_apart(dve, bn_done, n * TPB + (j + 1))
                dve.bn_aggr(stats[:, j, :], bn[:, j, :]).then_inc(stats_done, 1)

            def step(s):
                if not s.first:
                    mix_matrix(s.i, R, 0)
                    mix_matrix(s.i, R, 1)
                    result(s.i - 1, 1)
                running_max(s, 0)
                if not s.last:
                    difference(s.i + 1, s.batch + 1 if s.half == 1 else None)
                clip(s, 0)
                if not s.last:
                    mix_matrix(s.i + 1, K, 0)
                if not s.first:
                    add_rows(s.i - 1, 0)
                    statistics(s.i - 1, 0)
                    add_rows(s.i - 1, 1)
                scan_den(s, 0)
                if not s.last:
                    mix_matrix(s.i + 1, K, 1)
                if not s.first:
                    add_rows(s.i - 1, 2)
                    statistics(s.i - 1, 1)
                    statistics(s.i - 1, 2)
                scan_num(s, 0)
                if not s.first:
                    add_rows(s.i - 1, 3)
                    aggregate(s.i - 1, 0)
                    statistics(s.i - 1, 3)
                    aggregate(s.i - 1, 1)
                    aggregate(s.i - 1, 2)
                    aggregate(s.i - 1, 3)
                    shift(s.i - 1)
                leave(s, 0)
                running_max(s, 1)
                clip(s, 1)
                if not s.last:
                    mix_matrix(s.i + 1, V, 0)
                scan_den(s, 1)
                denominator(s.i, 0)
                if not s.last:
                    mix_matrix(s.i + 1, V, 1)
                scan_num(s, 1)
                leave(s, 1)
                if s.last:
                    denominator(s.i, 1)
                    try_guess(dve, s.i, 0)
                result(s.i, 0)
                if not s.last:
                    denominator(s.i, 1)

            cs = [dve.memset(zero_row[:], 0.0), dve.memset(start_state[:], 0.0),
                  dve.memset(eps_t[:], EPS), dve.memset(cap_t[:], -LN_SHIFT * LN2)]
            cs[-1].then_inc(consts_set, 1)
            dve.wait_ge(consts_set, 1)
            dve.memset(start_state[:, SQ, :], START)
            dve.wait_ge(ident_zero, 2)
            dve.tensor_scalar(part8[:], part[:], float(EXPERTS), float(EXPERTS), ALU.is_ge, ALU.mult).then_inc(vec_ready, 1)
            dve.tensor_scalar(sel_bo[:], part[0:BIAS_ROWS, 0:1].to_broadcast([BIAS_ROWS, P]), float(2 * EXPERTS), None,
                              ALU.is_ge).then_inc(sel_ready, 1)
            dve.wait_ge(vec_ready, 1)
            dve.tensor_tensor(part8[:], part[:], part8[:], ALU.subtract).then_inc(vec_ready, 1)
            dve.wait_ge(vec_ready, 2)
            dve.wait_ge(sel_ready, 1)
            dve.wait_ge(vec_loaded, 16)
            dve.tensor_scalar(nbr[:], vec[:, VEC_BR, :], -1.0, None, ALU.mult).then_inc(vec_ready, 1)
            dve.wait_ge(decay_exp, 1)
            dve.tensor_scalar(wdec[:], wdec[:], -1.0, None, ALU.mult).then_inc(vec_ready, 1)
            dve.wait_ge(vec_ready, 4)
            dve.tensor_tensor(uw[:], vec[:, VEC_FIRST, :], wdec[:], ALU.add).then_inc(vec_ready, 1)
            dve.wait_ge(vec_ready, 5)
            dve.sem_inc(y_taken, 2)
            dve.memset(xb[:, :, 0:1], 0.0).then_inc(x_padded, 1)
            dve.wait_ge(x_padded, 1)
            for hp in range(2):
                half = slice(2 * hp, 2 * hp + 2)
                dve.wait_ge(x_first[hp], 16)
                dve.tensor_tensor(diff[:, half], xb[:, half, 1:], xb[:, half, 0:TB], ALU.subtract).then_inc(diffed, 1)
                dve.wait_ge(diffed, hp + 1)
                mix_matrix(0, K, hp)
            for hp in range(2):
                dve.wait_ge(mixed_hi, hp + 1)
                dve.tensor_tensor(mixed[:, K, LO, 2 * hp:2 * hp + 2, :], unsplit[:, K, LO, 2 * hp:2 * hp + 2, :],
                                  mixed[:, K, HI, 2 * hp:2 * hp + 2, :].bitcast(F32),
                                  ALU.subtract).then_inc(mixed_lo, 1)
            for m in (V, R):
                mix_matrix(0, m, 0)
                mix_matrix(0, m, 1)
            dve.wait_ge(b_hi, 2)
            dve.tensor_tensor(b_split[:, LO], b_raw[:], b_split[:, HI].bitcast(F32), ALU.subtract).then_inc(b_lo, 1)
            dve.tensor_tensor(bo_split[:, LO], bo_raw[:], bo_split[:, HI].bitcast(F32), ALU.subtract).then_inc(b_lo, 1)
            dve.wait_ge(bias_moved, 64)
            dve.wait_ge(zero_stored, 16)
            walk(dve, step, dve.Fori)
            last = BLOCKS - 1
            try_guess(dve, last, 1)
            rwkv_lo(dve, last, 0)
            result(last, 1)
            rwkv_lo(dve, last, 1)

            expert_lo(dve, 2)

            def shift_last(j):
                dve.wait_ge(rstd_ready, last + (j + 1))
                dve.scalar_tensor_tensor(out=nmr[:, j:j + 1], in0=stats[:, j, 0:1], scalar=-1.0, in1=rstd[:, j:j + 1],
                                         op0=ALU.mult, op1=ALU.mult).then_inc(nmr_ready, 1)

            for j in range(TPB):
                add_rows(last, j, y_banks[j])
                statistics(last, j)
                if j:
                    shift_last(j - 1)
                aggregate(last, j)
            shift_last(TPB - 1)

            chain = [0]

            def link(ins):
                chain[0] += 1
                ins.then_inc(routed, 1)
                dve.wait_ge(routed, chain[0])

            def over(t, shape):
                return t.to_broadcast(shape)

            te_shape = [P, TILES, EXPERTS]
            dve.wait_ge(logits_done, TILES)
            dve.wait_ge(route_const, 1)
            link(dve.tensor_reduce(mx[:], lg_ps[:], AX_X, ALU.max))
            hot_v, place_v = hot[:].rearrange("p e t -> p t e"), place_e[:].rearrange("p e t -> p t e")
            dve.tensor_tensor(lg[:], lg_ps[:], over(mx[:, :, None], te_shape), ALU.subtract).then_inc(shifted, 1)
            dve.wait_ge(shifted, 1)
            link(dve.scalar_tensor_tensor(out=place_v, in0=lg[:], scalar=0.0, in1=over(rank8[:, None, :], te_shape),
                                          op0=ALU.is_ge, op1=ALU.mult))
            link(dve.tensor_reduce(chosen[:], place_v, AX_X, ALU.max))
            dve.tensor_tensor(hot_v, over(chosen[:, :, None], te_shape), over(rank8[:, None, :], te_shape),
                              ALU.is_equal).then_inc(hot_ready, 1)
            dve.wait_ge(hot_ready, 1)
            dve.wait_ge(gate_exp, 1)
            link(dve.tensor_reduce(sums[:], gate_e[:], AX_X, ALU.add))
            link(dve.reciprocal(gate[:], sums[:]))
            link(dve.tensor_copy(gate_parts[:, HI], gate[:]))
            dve.tensor_tensor(gate_parts[:, LO], gate[:], gate_parts[:, HI].bitcast(F32), ALU.subtract).then_inc(gate_split, 1)
            flat = lambda t: t[:].rearrange("p e t -> p (e t)")
            n_te = EXPERTS * TILES
            dve.wait_ge(counted, 1)
            link(dve.tensor_tensor_scan(flat(work), flat(segment), y_ps[:, 1, 0:n_te], 0.0, ALU.mult, ALU.add))
            link(dve.tensor_tensor(place_e[:], over(work[:, :, TILES - 1:TILES], [P, EXPERTS, TILES]), steps[:], ALU.is_gt))
            link(dve.tensor_reduce(ntiles[:], place_e[:], AX_X, ALU.add))
            link(dve.tensor_tensor_scan(ends[:], over(filled[:, 0:1], [P, EXPERTS]), ntiles[:], 0.0, ALU.mult, ALU.add))
            link(dve.tensor_tensor(starts[:], ends[:], ntiles[:], ALU.subtract))
            link(dve.tensor_tensor(flat(work), flat(work), y_ps[:, 0, 0:n_te], ALU.add))
            link(dve.scalar_tensor_tensor(out=work[:], in0=over(starts[:, :, None], [P, EXPERTS, TILES]), scalar=float(P),
                                          in1=work[:], op0=ALU.mult, op1=ALU.add))
            link(dve.tensor_tensor(work[:], work[:], hot[:].bitcast(F32), ALU.mult))
            link(dve.tensor_reduce(dest[:], work[:].rearrange("p e t -> p t e"), AX_X, ALU.add))
            link(dve.tensor_copy(dest_i[:, 0], dest[:]))
            link(dve.tensor_scalar(dest_i[:, 1], dest_i[:, 0], 7, None, ALU.logical_shift_right))
            link(dve.tensor_scalar(dest_i[:, 2], dest_i[:, 0], P - 1, None, ALU.bitwise_and))
            link(dve.tensor_copy(dest_f[:], dest_i[:, 1:3]))
            dve.tensor_tensor(place_k[:], over(dest_f[:, 0, :, None], [P, TILES, LISTS]),
                              over(iota_k[:, None, :], [P, TILES, LISTS]), ALU.is_equal).then_inc(tile_placed, 1)
            dve.wait_ge(tile_placed, 1)
            dve.tensor_tensor(place_list[:, :, 0, :], place_k[:], over(token1[:, :, None], [P, TILES, LISTS]), ALU.mult)
            for t in range(0, TILES, PART):
                part_shape = [P, PART, P]
                dve.tensor_tensor(place_q[:, t:t + PART, :], over(dest_f[:, 1, t:t + PART, None], part_shape),
                                  over(iota_q[:, None, :], part_shape), ALU.is_equal).then_inc(placed, 1)
            for j in range(TPB):
                dve.wait_ge(row_stored[j], BLOCKS * 16)
            link(dve.tensor_tensor(after[:], over(iota_k[:, 0:SORTED, None], [P, SORTED, EXPERTS]),
                                   over(ends[:, None, :], [P, SORTED, EXPERTS]), ALU.is_ge))
            link(dve.tensor_reduce(tile_e[:], after[:], AX_X, ALU.add))
            link(dve.tensor_scalar(tile_e[:], tile_e[:], float(EXPERTS - 1), None, ALU.min))
            dve.tensor_copy(tile_ei[:], tile_e[:]).then_inc(tiles_ready, 1)
            dve.wait_ge(listed, 1)
            link(dve.tensor_scalar(empty[:], list_ps[:, 0:SORTED], 0.0, float(TOKENS + 1), ALU.is_equal, ALU.mult))
            dve.scalar_tensor_tensor(out=ids[:], in0=list_ps[:, 0:SORTED], scalar=-1.0, in1=empty[:],
                                     op0=ALU.add, op1=ALU.add).then_inc(ids_ready, 1)
            link(dve.tensor_copy(gates[:], list_ps[:, LISTS:LISTS + SORTED]))
            link(dve.tensor_tensor(gates[:], gates[:], list_ps[:, 2 * LISTS:2 * LISTS + SORTED], ALU.add))

            def turned_split_lo(k, n):
                dve.wait_ge(turned_hi, k + 1)
                dve.tensor_tensor(xgT[:, n % 3, LO], turned_ps[n % 2], xgT[:, n % 3, HI].bitcast(F32), ALU.subtract).then_inc(turned_lo, 1)
                wait(dve, expert_filled, k - 2)
                dve.tensor_scalar(sel_e[:, n % 3], tile_e[0:BIAS_ROWS, bass.ds(k, 1)].to_broadcast([BIAS_ROWS, P]),
                                  part8[0:BIAS_ROWS, :], None, ALU.is_equal).then_inc(sel_set, 1)

            def add_gathered(k, r, n):
                dve.wait_ge(expert_filled, k + 1)
                wait(dve, scattered[n], r * 16)
                dve.scalar_tensor_tensor(out=yo[:, n], in0=y_ps[:, n % 2, :], scalar=gates[:, bass.ds(k, 1)],
                                         in1=xg[:, n], op0=ALU.mult, op1=ALU.add).then_inc(y_taken, 1)
                dve.wait_ge(y_taken, k + (TILES + 3))
                dve.bn_stats(bn2[:, n, :], yo[:, n]).then_inc(bn2_done, 1)
                wait_apart(dve, bn2_done, k + 1)
                dve.bn_aggr(stats2[:, n, :], bn2[:, n, :]).then_inc(stats2_done, 1)

            def shift2(k, n):
                dve.wait_ge(rstd2_ready, k + 1)
                dve.scalar_tensor_tensor(out=nmr2[:, n:n + 1], in0=stats2[:, n, 0:1], scalar=-1.0, in1=rstd2[:, n:n + 1],
                                         op0=ALU.mult, op1=ALU.mult).then_inc(nmr2_ready, 1)

            for k in range(3):
                turned_split_lo(k, k)
            add_gathered(0, 0, 0)
            rounds = (SORTED - 3) // RING

            def step(r, n):
                turned_split_lo(r * RING + (n + 3), (n + 3) % RING)
                shift2(r * RING + n, n)
                add_gathered(r * RING + (n + 1), r + (n + 1) // RING, (n + 1) % RING)

            for n in range(RING):
                step(0, n)
            with dve.Fori(1, rounds) as r:
                for n in range(RING):
                    step(r, n)
            for k in range(rounds * RING, SORTED):
                if k + 3 < SORTED:
                    turned_split_lo(k + 3, (k + 3) % RING)
                shift2(k, k % RING)
                if k + 1 < SORTED:
                    add_gathered(k + 1, (k + 1) // RING, (k + 1) % RING)


def kernel(**inputs):
    import numpy as np
    import concourse.bacc as bacc
    from concourse.bass_utils import run_bass_kernel_spmd

    a = {name.replace("L0_", ""): np.asarray(value) for name, value in inputs.items()}
    by_partition = lambda name: a["attn_" + name].reshape(CH, P).T
    arrays = {
        "x": a["attn_x"],
        "xT": a["attn_x"].transpose(0, 2, 1),
        "w_square": np.stack([a["attn_Wk"].T, a["attn_Wv"].T, a["attn_Wr"].T, a["attn_Wo"].T]),
        "w_experts": a["ffn_W"].transpose(0, 2, 1),
        "vectors": np.stack([by_partition(n) for n in ("bk", "bv", "br", "tmk", "tmv", "tmr", "time_decay", "time_first")], axis=1),
        "bo": a["attn_bo"].reshape(1, H),
        "b_experts": a["ffn_b"],
        "wg": a["ffn_wg"],
    }
    arrays = {name: np.ascontiguousarray(value) for name, value in arrays.items()}
    nc = bacc.Bacc("TRN2", target_bir_lowering=False, num_devices=1)
    aps = [nc.dram_tensor(name, value.shape, mybir.dt.from_np(value.dtype), kind="ExternalInput").ap()
           for name, value in arrays.items()]
    out = nc.dram_tensor("out", (BATCH, TIME, H), F32, kind="ExternalOutput").ap()
    build(nc, *aps, out)
    result = run_bass_kernel_spmd(nc, [arrays], core_ids=[0])
    return result.results[0]["out"]
```
